# Optimizing a Trainium2 kernel written in Bass

```python
import numpy as np
import jax
import jax.numpy as jnp

def _softmax(x, axis=-1):
    return jax.nn.softmax(x, axis=axis)

def _gelu(x):
    return jax.nn.gelu(x, approximate=True)

def _silu(x):
    return jax.nn.silu(x)

def _sigmoid(x):
    return jax.nn.sigmoid(x)

def _layernorm(x, axis=-1, eps=1e-05):
    m = jnp.mean(x, axis=axis, keepdims=True)
    v = jnp.var(x, axis=axis, keepdims=True)
    return (x - m) / jnp.sqrt(v + eps)

def _scatter_add(tgt, idx, src, axis=0):
    return tgt.at[idx].add(src)

def _segment_sum(src, seg, n):
    return jax.ops.segment_sum(src, seg, n)
kernel_name = 'mk_gnn_resnorm_d2_gnn_r8_3ee653'

def setup_inputs(seed: int=0):
    np.random.seed(seed)
    _w = jnp.asarray

    def _rec_inputs():
        import jax
        import jax.numpy as jnp
        _gk = jax.random.key(seed)
        x = -0.0005121 + 1.001 * jax.random.normal(jax.random.fold_in(_gk, 1), (6250, 64), jnp.float32)
        src = jax.random.randint(jax.random.fold_in(_gk, 2), (200000,), 0, 6250, jnp.int32)
        dst = jax.random.randint(jax.random.fold_in(_gk, 3), (200000,), 0, 6250, jnp.int32)
        _o = jnp.argsort(dst, stable=True)
        src = src[_o]
        dst = dst[_o]
        edge_type_32 = jax.random.randint(jax.random.fold_in(_gk, 13), (200000,), 0, 32, jnp.int32)
        edge_weight = jax.random.uniform(jax.random.fold_in(_gk, 14), (200000,), jnp.float32, 0.0, 0.999996)
        return (x, src, dst, edge_type_32, edge_weight)
    x, src, dst, edge_type_32, edge_weight = _rec_inputs()

    def _L0_gnn_setup():
        import jax, jax.numpy as jnp
        import numpy as np
        N = 6250
        E = 100000
        IN = 64
        OUT = 64
        R = 32
        B = 4
        key = jax.random.key(seed)
        ks = jax.random.split(key, 8)
        h = jax.random.normal(ks[0], (N, IN), dtype=jnp.float32)
        weight = jax.random.normal(ks[1], (B, IN, OUT), dtype=jnp.float32) * (1.0 / np.sqrt(IN))
        w_comp = jax.random.normal(ks[2], (R, B), dtype=jnp.float32) * (1.0 / np.sqrt(B))
        bias = jax.random.normal(ks[3], (OUT,), dtype=jnp.float32) * 0.02
        src = jax.random.randint(ks[4], (E,), 0, N)
        dst = jax.random.randint(ks[5], (E,), 0, N)
        etype = jax.random.randint(ks[6], (E,), 0, R)
        edge_norm = jax.random.uniform(ks[7], (E,), dtype=jnp.float32)
        return {'h': h, 'weight': weight, 'w_comp': w_comp, 'bias': bias, 'edge_norm': edge_norm, 'src': src, 'dst': dst, 'etype': etype}
    _L0_gnn_all = _L0_gnn_setup()
    _L0_gnn_in = {k: v for k, v in _L0_gnn_all.items() if k in ('weight', 'w_comp', 'bias')}
    del _L0_gnn_all

    def _L1_gnn_setup():
        import jax, jax.numpy as jnp
        import numpy as np
        N_NODES = 12500
        N_EDGES = 400000
        D_IN = 64
        D_OUT = 64
        key = jax.random.key(seed)
        k0, k1, k2, k3 = jax.random.split(key, 4)
        x = jax.random.normal(k0, (N_NODES, D_IN), dtype=jnp.float32)
        edge_index = jax.random.randint(k1, (2, N_EDGES), 0, N_NODES, dtype=jnp.int64)
        edge_weight = jax.random.uniform(k2, (N_EDGES,), dtype=jnp.float32)
        W = jax.random.normal(k3, (D_IN, D_OUT), dtype=jnp.float32) / jnp.sqrt(jnp.float32(D_IN))
        b = jnp.zeros((D_OUT,), dtype=jnp.float32)
        return {'x': x, 'edge_index': edge_index, 'edge_weight': edge_weight, 'W': W, 'b': b}
    _L1_gnn_all = _L1_gnn_setup()
    _L1_gnn_in = {k: v for k, v in _L1_gnn_all.items() if k in ('W', 'b')}
    del _L1_gnn_all
    return {'x': x, 'src': src, 'dst': dst, 'edge_type_32': edge_type_32, 'edge_weight': edge_weight, 'L0_gnn_weight': _L0_gnn_in['weight'], 'L0_gnn_w_comp': _L0_gnn_in['w_comp'], 'L0_gnn_bias': _L0_gnn_in['bias'], 'L1_gnn_W': _L1_gnn_in['W'], 'L1_gnn_b': _L1_gnn_in['b']}

def reference(x, src, dst, edge_type_32, edge_weight, L0_gnn_weight, L0_gnn_w_comp, L0_gnn_bias, L1_gnn_W, L1_gnn_b):
    import jax
    import jax.numpy as jnp

    def _L0_gnn_ref(h, weight, w_comp, bias, edge_norm, src, dst, etype):
        import jax, jax.numpy as jnp
        import numpy as np
        N = 6250
        E = 100000
        IN = 64
        OUT = 64
        R = 32
        B = 4
        coeff = w_comp[etype]
        h_src = h[src]
        msg_b = jnp.einsum('ei,bio->ebo', h_src, weight)
        msg = jnp.einsum('ebo,eb->eo', msg_b, coeff)
        msg = msg * edge_norm[:, None]
        agg = jax.ops.segment_sum(msg, dst, num_segments=N)
        return jax.nn.relu(agg + bias)

    def _L1_gnn_ref(x, edge_index, edge_weight, W, b):
        import jax, jax.numpy as jnp
        import numpy as np
        N_NODES = 12500
        N_EDGES = 400000
        D_IN = 64
        D_OUT = 64
        N = x.shape[0]
        src, dst = (edge_index[0], edge_index[1])
        loop = jnp.arange(N, dtype=src.dtype)
        src = jnp.concatenate([src, loop])
        dst = jnp.concatenate([dst, loop])
        ew = jnp.concatenate([edge_weight.astype(x.dtype), jnp.ones((N,), dtype=x.dtype)])
        deg = jax.ops.segment_sum(ew, dst, num_segments=N)
        deg_inv = jnp.where(deg > 0, 1.0 / deg, 0.0)
        norm = deg_inv[dst] * ew
        h = x @ W
        msg = norm[:, None] * h[src]
        out = jax.ops.segment_sum(msg, dst, num_segments=N)
        return out + b
    edge_index = jnp.stack([src, dst])
    x = _layernorm(x + _L0_gnn_ref(x, L0_gnn_weight, L0_gnn_w_comp, L0_gnn_bias, edge_weight, src, dst, edge_type_32), axis=-1)
    x = _layernorm(x + _L1_gnn_ref(x, edge_index, edge_weight, L1_gnn_W, L1_gnn_b), axis=-1)
    return x

_drawn_inputs = setup_inputs


def setup_inputs(seed=0):
    import zlib

    import numpy as np

    out = dict(_drawn_inputs(seed))
    spreads = {'L1_gnn_b': (0.0, 0.1)}
    factors = {'L0_gnn_bias': 6.124}
    for name, (base, spread) in spreads.items():
        noise = np.random.default_rng([zlib.crc32(name.encode()), seed]).standard_normal(out[name].shape)
        drawn = base * np.exp(spread * noise) if base else spread * noise
        out[name] = jnp.asarray(drawn.astype(out[name].dtype))
    for name, factor in factors.items():
        out[name] = (out[name] * factor).astype(out[name].dtype)
    return out
```

```python
import concourse.bass as bass
from concourse import mybir
from contextlib import ExitStack


N = 6250
E = 200000
D = 64
R = 32
B = 4
P = 128
CH = 8
U = 3
WIN = 48
CHUNKS = -(-E // P)
ITERS = CHUNKS // (CH * U)
TAIL = CHUNKS - ITERS * CH * U
GROUPS = ITERS * U + 1
BLOCKS = -(-CHUNKS // P)
LEFT = CHUNKS - (BLOCKS - 1) * P
TURN = 4
STEPS = (ITERS + 1) * U
TILES = -(-N // P)
NPAD = TILES * P + WIN
BATCH = 7
BATCHES = TILES // BATCH
EXTRA = -(-N // WIN)
EPS = 1e-5
TINY = 1.1754943508222875e-38
assert 0 < TAIL <= CH and TILES == BATCH * BATCHES and GROUPS <= 2 * P
LAST = N - (TILES - 1) * P


def gnn_two_layers(nc, x, src, dst, etype, eweight, w0, w_comp, bias0, w1, bias1, out):
    f32 = mybir.dt.float32
    i32 = mybir.dt.int32
    ALU = mybir.AluOpType
    ACT = mybir.ActivationFunctionType
    AX = mybir.AxisListType

    table = nc.dram_tensor("x1_table", (TILES * P, D), f32, kind="Internal").ap()
    edge_arrays = (src, dst, etype, eweight)
    SRC, DST, TYPE, WEIGHT = range(4)

    ctx = ExitStack()
    with ctx:
        def sb(name, shape, dt=f32):
            return ctx.enter_context(nc.sbuf_tensor(name, shape, dt))

        def pb(name, shape):
            return ctx.enter_context(nc.psum_tensor(name, shape, f32))

        def sem(name):
            return ctx.enter_context(nc.semaphore(name))

        ident = sb("ident", [P, P])
        ones = sb("ones", [P, P])
        type_iota_sb = sb("type_iota_sb", [P, R])
        win_iota_sb = sb("win_iota_sb", [P, WIN])
        win_steps = sb("win_steps", [P, EXTRA])
        lo = sb("lo", [P, 2])
        hi = sb("hi", [P, 2])
        span = sb("span", [P, 2])
        first_base = sb("first_base", [P, GROUPS])
        base = sb("base", [1, GROUPS])
        base_int = sb("base_int", [1, GROUPS], i32)
        max_span = sb("max_span", [P, 1])
        further = sb("further", [P, EXTRA])
        n_further = sb("n_further", [P, 1])
        n_passes = sb("n_passes", [1, 1], i32)
        edges = sb("edges", [P, 4, CHUNKS])
        local_dst = sb("local_dst", [P, CHUNKS])
        idx = sb("idx", [P, U, CH], i32)
        gathered_rows = sb("gathered_rows", [P, U, CH, D + 16])
        type_hot = sb("type_hot", [P, U, CH, R])
        diag = type_hot[:, :, :, :].rearrange("p s c r -> p (s c r)")[:, 0:4 * P].rearrange("p (d q) -> p d q", d=4)
        type_hot_t = sb("type_hot_t", [P, 2, P])
        coef_w = sb("coef_w", [P, U, CH, B])
        factors = sb("factors", [P, U, CH, B, WIN])
        dst_by_group = factors[:, :, :, :, :].rearrange("p s c b w -> p (s c b w)")[:, 0:2 * P * CH] \
            .bitcast(i32).rearrange("p (h e) -> p h e", h=2)
        wc_blocks = sb("wc_blocks", [P, 4 * B])
        w0_sb = sb("w0_sb", [D + 1, B, D])
        w1_sb = sb("w1_sb", [D + 1, D + 1])
        bias1_bc = sb("bias1_bc", [P, D])
        x_nodes = sb("x_nodes", [P, TILES, D])
        edge_rows = sb("edge_rows", [P, 4, BLOCKS, P])
        room = edge_rows[:, :, :, :].rearrange("p a t e -> p (a t e)")
        x1_nodes = room[:, 0:TILES * (D + 1)].rearrange("p (t f) -> p t f", f=D + 1)
        y_nodes = room[:, TILES * (D + 1):TILES * (2 * D + 1)].rearrange("p (t f) -> p t f", f=D)
        acc0 = sb("acc0", [D + 1, B, NPAD])
        acc1 = acc0[:, 0, :]
        h_nodes = sb("h_nodes", [P, BATCH, D])
        stats = sb("stats", [P, BATCH, 6])
        mean_var = sb("mean_var", [P, BATCH, 2])
        var_eps = sb("var_eps", [P, BATCH])
        std = sb("std", [P, BATCH])
        rstd = sb("rstd", [P, BATCH])
        has_deg = sb("has_deg", [P, BATCH])
        safe_deg = sb("safe_deg", [P, BATCH])
        inv_deg = sb("inv_deg", [P, BATCH])

        types_ps = pb("types_ps", [P, 512])
        coefs_ps = pb("coefs_ps", [P, 512])
        turn_ps = [types_ps, coefs_ps]
        dve_ps = pb("dve_ps", [P, 512])
        type_iota = dve_ps[:, 0:R]
        win_iota = dve_ps[:, R:R + WIN]
        hits = dve_ps[:, 128:128 + CH * WIN].rearrange("p (c w) -> p c w", c=CH)
        sums_ps = [pb(f"sums_ps{s}", [P, 512]) for s in range(U)]
        node_ps = pb("node_ps", [P, 512])

        x_loaded = sem("x_loaded")
        params_loaded = sem("params_loaded")
        dst_loaded = sem("dst_loaded")
        consts_ready = sem("consts_ready")
        pool_step = sem("pool_step")
        params_zeroed = sem("params_zeroed")
        diag_ready = sem("diag_ready")
        bases_spread = sem("bases_spread")
        passes_ready = sem("passes_ready")
        start_step = sem("start_step")
        base_ready = sem("base_ready")
        rows_loaded = [sem(f"rows_loaded{a}") for a in range(4)]
        rows_are_float = [sem(f"rows_are_float{a}") for a in range(3)]
        rows_turned = sem("rows_turned")
        edges_ready = sem("edges_ready")
        idx_ready = sem("idx_ready")
        gathers_begun = sem("gathers_begun")
        rows_gathered = [sem(f"rows_gathered{s}") for s in range(U)]
        types_hot = sem("types_hot")
        types_turned = sem("types_turned")
        types_copied = sem("types_copied")
        coefs_ready = sem("coefs_ready")
        dst_local = sem("dst_local")
        hits_ready = sem("hits_ready")
        coefs_weighted = sem("coefs_weighted")
        factors_ready = sem("factors_ready")
        group_summed = sem("group_summed")
        window_added = sem("window_added")
        nodes_out = sem("nodes_out")
        nodes_read = sem("nodes_read")
        norm_step = sem("norm_step")
        var_ready = sem("var_ready")
        std_ready = sem("std_ready")
        x1_ready = sem("x1_ready")
        x1_turned = sem("x1_turned")
        self_added = sem("self_added")
        x1_stored = sem("x1_stored")
        y_ready = sem("y_ready")
        y_stored = sem("y_stored")
        bias_added = sem("bias_added")

        block = ctx.enter_context(nc.Block())

        N_PARAMS = 4 + 1 + 1 + 1 + 1
        WHOLE = 16 * CH
        PER_PASS = [ITERS * WHOLE + (16 * TAIL if s == 0 else 0) for s in range(U)]
        FREE = U

        def chunks_of(g):
            return TAIL if g == GROUPS - 1 else CH

        def weight_of(tail):
            return U if tail else 1

        @block.sync
        def _(sp):
            def load_rows(a):
                to = edge_rows[:, a, :, :] if a == WEIGHT else edge_rows[:, a, :, :].bitcast(i32)
                rows = edge_arrays[a].rearrange("(c e) -> c e", e=P)
                whole = (BLOCKS - 1) * P
                sp.dma_start(to[:, 0:BLOCKS - 1, :], rows[0:whole, :].rearrange("(t p) e -> p t e", p=P)).then_inc(rows_loaded[a], 16)
                sp.dma_start(to[0:LEFT, BLOCKS - 1, :], rows[whole:CHUNKS, :]).then_inc(rows_loaded[a], 16)

            sp.dma_start(dst_by_group[:, 0, :], dst[0:P * P * CH].rearrange("(g e) -> g e", g=P)).then_inc(dst_loaded, 16)
            rest = GROUPS - 1 - P
            sp.dma_start(dst_by_group[0:rest, 1, :],
                         dst[P * P * CH:(GROUPS - 1) * P * CH].rearrange("(g e) -> g e", g=rest)).then_inc(dst_loaded, 16)
            sp.dma_start(dst_by_group[rest:rest + 1, 1, :],
                         dst[(CHUNKS - CH) * P:CHUNKS * P].rearrange("(g e) -> g e", g=1)).then_inc(dst_loaded, 16)
            for a in (SRC, DST, TYPE, WEIGHT):
                load_rows(a)
            sp.wait_ge(params_zeroed, 1)
            for j in range(4):
                sp.dma_start(wc_blocks[R * j:R * j + R, B * j:B * j + B], w_comp[:, :]).then_inc(params_loaded, 16)
            sp.dma_start(w0_sb[0:D, :, :], w0.rearrange("b i o -> i b o")).then_inc(params_loaded, 16)
            sp.dma_start(w0_sb[D:D + 1, 0, :], bias0.rearrange("(a o) -> a o", a=1)).then_inc(params_loaded, 16)
            sp.dma_start(w1_sb[0:D, 0:D], w1[:, :]).then_inc(params_loaded, 16)
            sp.dma_start(bias1_bc[:, :], bias1.rearrange("(a o) -> a o", a=1).to_broadcast([P, D])).then_inc(params_loaded, 16)
            sp.dma_start(x_nodes[:, 0:TILES - 1, :], x[0:(TILES - 1) * P, :].rearrange("(t p) f -> p t f", p=P)).then_inc(x_loaded, 16)
            sp.dma_start(x_nodes[0:LAST, TILES - 1, :], x[(TILES - 1) * P:N, :]).then_inc(x_loaded, 16)
            for b in range(BATCHES):
                sp.wait_ge(x1_ready, b + 1)
                sp.dma_start(table[b * BATCH * P:(b + 1) * BATCH * P, :].rearrange("(t p) f -> p t f", p=P),
                             x1_nodes[:, b * BATCH:(b + 1) * BATCH, 0:D]).then_inc(x1_stored, 16)
            for b in range(BATCHES):
                sp.wait_ge(y_ready, b + 1)
                t0, t1 = b * BATCH, min((b + 1) * BATCH, TILES - 1)
                sp.dma_start(out[t0 * P:t1 * P, :].rearrange("(t p) f -> p t f", p=P),
                             y_nodes[:, t0:t1, :]).then_inc(y_stored, 16)
            sp.dma_start(out[(TILES - 1) * P:N, :], y_nodes[0:LAST, TILES - 1, :]).then_inc(y_stored, 16)
            sp.wait_ge(y_stored, 16 * (BATCHES + 1))

        @block.gpsimd
        def _(pool):
            nc.gpsimd.memset(ones[:, :], 1.0).then_inc(pool_step, 1)
            nc.gpsimd.memset(ident[:, :], 0.0).then_inc(pool_step, 1)
            pool.wait_ge(pool_step, 2)
            nc.gpsimd.affine_select(out=ident[:, :], in_=ident[:, :], compare_op=ALU.not_equal, fill=1.0, base=0,
                                    pattern=[[-1, P]], channel_multiplier=1).then_inc(consts_ready, 1)
            nc.gpsimd.iota(type_iota_sb[:, :], pattern=[[1, R]], base=0, channel_multiplier=0,
                           allow_small_or_imprecise_dtypes=True).then_inc(consts_ready, 1)
            nc.gpsimd.iota(win_iota_sb[:, :], pattern=[[1, WIN]], base=0, channel_multiplier=0,
                           allow_small_or_imprecise_dtypes=True).then_inc(consts_ready, 1)
            nc.gpsimd.iota(win_steps[:, :], pattern=[[WIN, EXTRA]], base=WIN, channel_multiplier=0,
                           allow_small_or_imprecise_dtypes=True).then_inc(consts_ready, 1)
            nc.gpsimd.memset(gathered_rows[:, :, :, D:D + 1], 1.0).then_inc(consts_ready, 1)
            for a in (DST, TYPE):
                pool.wait_ge(rows_loaded[a], 32)
                rows = edge_rows[:, a, :, :]
                nc.gpsimd.tensor_copy(rows[:, 0:BLOCKS - 1, :], rows[:, 0:BLOCKS - 1, :].bitcast(i32)).then_inc(rows_are_float[a], 1)
                nc.gpsimd.tensor_copy(rows[0:LEFT, BLOCKS - 1, :], rows[0:LEFT, BLOCKS - 1, :].bitcast(i32)).then_inc(rows_are_float[a], 1)
            pool.wait_ge(passes_ready, 1)
            passes = pool.value_load(n_passes[0:1, 0:1], min_val=1, max_val=EXTRA + 1)

            def gather_group(step, s, chunks, rows):
                pool.wait_ge(idx_ready, step + 1)
                pool.sem_inc(gathers_begun, 1)
                for j in range(chunks):
                    pool.indirect_dma_start(gathered_rows[:, s, j, 0:D], None, rows,
                                            bass.IndirectOffsetOnAxis(ap=idx[:, s, j:j + 1], axis=0)
                                            ).then_inc(rows_gathered[s], 16)

            for layer in range(2):
                rows = table[:, :] if layer else x[:, :]
                if layer:
                    pool.wait_ge(x1_stored, 16 * BATCHES)
                with pool.Fori(0, passes) as k:
                    step0 = (k + passes if layer else k) * STEPS
                    with pool.Fori(0, ITERS) as i:
                        for s in range(U):
                            gather_group(step0 + i * U + s, s, CH, rows)
                    gather_group(step0 + ITERS * U, 0, TAIL, rows)

        @block.scalar
        def _(act):
            act.wait_ge(rows_loaded[SRC], 32)
            rows = edge_rows[:, SRC, :, :]
            nc.scalar.copy(rows[:, 0:BLOCKS - 1, :], rows[:, 0:BLOCKS - 1, :].bitcast(i32)).then_inc(rows_are_float[SRC], 1)
            nc.scalar.copy(rows[0:LEFT, BLOCKS - 1, :], rows[0:LEFT, BLOCKS - 1, :].bitcast(i32)).then_inc(rows_are_float[SRC], 1)
            turned = 0
            for a in (SRC, DST, TYPE, WEIGHT):
                for t in range(0, BLOCKS, TURN):
                    n = min(TURN * P, CHUNKS - t * P)
                    act.wait_ge(rows_turned, turned + 1)
                    nc.scalar.copy(edges[:, a, t * P:t * P + n], turn_ps[turned % 2][:, 0:n]).then_inc(edges_ready, 1)
                    turned += 1
            act.wait_ge(edges_ready, turned)
            act.wait_ge(passes_ready, 1)
            passes = act.value_load(n_passes[0:1, 0:1], min_val=1, max_val=EXTRA + 1)

            def index_group(layer, step, g, s, chunks, count):
                act.wait_ge(group_summed, step + 1)
                nc.scalar.copy(idx[:, s, 0:chunks], edges[:, SRC, bass.ds(g * CH, chunks)]).then_inc(idx_ready, count)
                if layer == 0:
                    act.wait_ge(types_turned, step + 1)
                    for h in range(-(-chunks // 4)):
                        n = min(4, chunks - 4 * h) * R
                        last = nc.scalar.copy(type_hot_t[0:n, h, :], types_ps[0:n, h * P:h * P + P])
                    last.then_inc(types_copied, count)

            for layer in range(2):
                if layer:
                    for b in range(BATCHES):
                        act.wait_ge(var_ready, b + 1)
                        nc.scalar.activation(std[:, :], var_eps[:, :], ACT.Sqrt).then_inc(std_ready, 1)
                with act.Fori(0, passes) as k:
                    step0 = (k + passes if layer else k) * STEPS
                    with act.Fori(0, ITERS) as i:
                        for s in range(U):
                            index_group(layer, step0 + i * U + s, i * U + s, s, CH, 1)
                    index_group(layer, step0 + ITERS * U, ITERS * U, 0, TAIL, U)
            for b in range(BATCHES):
                act.wait_ge(var_ready, BATCHES + b + 1)
                nc.scalar.activation(std[:, :], var_eps[:, :], ACT.Sqrt).then_inc(std_ready, 1)

        @block.tensor
        def _(pe):
            pe.sem_inc(group_summed, FREE)
            pe.wait_ge(consts_ready, 5)
            turned = 0
            for a in (SRC, DST, TYPE, WEIGHT):
                if a == WEIGHT:
                    pe.wait_ge(rows_loaded[a], 32)
                else:
                    pe.wait_ge(rows_are_float[a], 2)
                for t0 in range(0, BLOCKS, TURN):
                    if turned >= 2:
                        pe.wait_ge(edges_ready, turned - 1)
                    for t in range(t0, min(t0 + TURN, BLOCKS)):
                        n = min(P, CHUNKS - t * P)
                        last = nc.tensor.transpose(turn_ps[turned % 2][:, (t - t0) * P:(t - t0) * P + n],
                                                   edge_rows[0:n, a, t, :], ident[0:n, 0:n])
                    last.then_inc(rows_turned, 1)
                    turned += 1
            pe.wait_ge(edges_ready, turned)
            pe.wait_ge(diag_ready, 4)
            for h in range(2):
                n = P if h == 0 else GROUPS - P
                nc.tensor.matmul(node_ps[:, P * h:P * h + n], ones[:, :], diag[:, h, 0:n], start=True, stop=True)
                last = nc.tensor.matmul(node_ps[:, 256 + P * h:256 + P * h + n], ones[:, :], diag[:, 2 + h, 0:n],
                                        start=True, stop=True)
            last.then_inc(bases_spread, 1)
            pe.wait_ge(params_loaded, 16 * N_PARAMS)
            pe.wait_ge(passes_ready, 1)
            passes = pe.value_load(n_passes[0:1, 0:1], min_val=1, max_val=EXTRA + 1)

            def look_up_coefs(step, s, chunks, count):
                pe.wait_ge(types_hot, step + 1)
                for h in range(-(-chunks // 4)):
                    n = min(4, chunks - 4 * h)
                    last = nc.tensor.transpose(types_ps[0:n * R, h * P:h * P + P],
                                               type_hot[:, s, 4 * h:4 * h + n, :].rearrange("p c r -> p (c r)"),
                                               ident[:, :])
                last.then_inc(types_turned, count)
                pe.wait_ge(types_copied, step + 1)
                pe.wait_ge(coefs_weighted, step + 1)
                for h in range(-(-chunks // 4)):
                    n = min(4, chunks - 4 * h)
                    last = nc.tensor.matmul(coefs_ps[:, 4 * h * B:(4 * h + n) * B], type_hot_t[0:n * R, h, :],
                                            wc_blocks[0:n * R, 0:n * B], start=True, stop=True)
                last.then_inc(coefs_ready, count)

            def sum_group(layer, step, s, use, chunks, count):
                pe.wait_ge(rows_gathered[s], use)
                pe.wait_ge(factors_ready, step + 2)
                pe.wait_ge(window_added, step + 1)
                for j in range(chunks):
                    if layer == 0:
                        last = nc.tensor.matmul(sums_ps[s][0:D, 0:B * WIN], gathered_rows[:, s, j, 0:D],
                                                factors[:, s, j, :, :].rearrange("p b w -> p (b w)"),
                                                start=(j == 0), stop=(j == chunks - 1))
                    else:
                        last = nc.tensor.matmul(sums_ps[s][0:D + 1, 0:WIN], gathered_rows[:, s, j, 0:D + 1],
                                                factors[:, s, j, 0, :], start=(j == 0), stop=(j == chunks - 1))
                last.then_inc(group_summed, count)

            for layer in range(2):
                with pe.Fori(0, passes) as k:
                    kk = k + passes if layer else k
                    step0 = kk * STEPS
                    use0 = [kk * PER_PASS[s] for s in range(U)]

                    def front(i, s, chunks, count):
                        if layer == 0:
                            look_up_coefs(step0 + i * U + s, s, chunks, count)

                    def back(i, s, chunks, count):
                        sum_group(layer, step0 + i * U + s, s, use0[s] + i * WHOLE + 16 * chunks, chunks, count)

                    front(0, 0, CH, 1)
                    front(0, 1, CH, 1)
                    front(0, 2, CH, 1)
                    back(0, 0, CH, 1)
                    with pe.Fori(1, ITERS) as i:
                        for s in range(U):
                            front(i, s, CH, 1)
                            if s < 2:
                                back(i - 1, s + 1, CH, 1)
                            else:
                                back(i, 0, CH, 1)
                    front(ITERS, 0, TAIL, U)
                    back(ITERS - 1, 1, CH, 1)
                    back(ITERS - 1, 2, CH, 1)
                    back(ITERS, 0, TAIL, U)
                pe.wait_ge(window_added, (passes * 2 if layer else passes) * STEPS + FREE)
                for b in range(BATCHES):
                    bank = sums_ps[b % 2]
                    if b >= 2 or layer:
                        pe.wait_ge(nodes_read, BATCHES * layer + b - 1)
                    for t in range(BATCH):
                        cols = slice((b * BATCH + t) * P, (b * BATCH + t + 1) * P)
                        if layer == 0:
                            for c in range(B):
                                kd = D + 1 if c == 0 else D
                                last = nc.tensor.matmul(bank[:, t * D:(t + 1) * D], acc0[0:kd, c, cols],
                                                        w0_sb[0:kd, c, :], start=(c == 0), stop=(c == B - 1))
                        else:
                            last = nc.tensor.matmul(bank[:, t * (D + 1):(t + 1) * (D + 1)], acc1[:, cols], w1_sb[:, :],
                                                    start=True, stop=True)
                    last.then_inc(nodes_out, 1)
                if layer == 0:
                    for t in range(TILES):
                        if t % BATCH == 0:
                            pe.wait_ge(x1_ready, t // BATCH + 1)
                        if t % 4 == 0 and t >= 4:
                            pe.wait_ge(self_added, t // 4)
                        last = nc.tensor.transpose(node_ps[0:D + 1, (t % 4) * P:(t % 4 + 1) * P], x1_nodes[:, t, :], ident[:, :])
                        if t % 4 == 3 or t == TILES - 1:
                            last.then_inc(x1_turned, 1)

        @block.vector
        def _(dve):
            nc.vector.memset(x_nodes[:, TILES - 1, :], 0.0)
            nc.vector.memset(wc_blocks[:, :], 0.0)
            nc.vector.memset(w1_sb[0:D, D:D + 1], 0.0)
            nc.vector.memset(w1_sb[D:D + 1, 0:D], 0.0)
            nc.vector.memset(w1_sb[D:D + 1, D:D + 1], 1.0).then_inc(params_zeroed, 1)
            dve.sem_inc(window_added, FREE)
            dve.sem_inc(coefs_weighted, 1)
            dve.sem_inc(factors_ready, 1)

            nc.vector.memset(lo[:, 1:2], 0.0).then_inc(start_step, 1)
            nc.vector.memset(hi[:, 1:2], 0.0).then_inc(start_step, 1)
            dve.wait_ge(start_step, 2)
            dve.wait_ge(dst_loaded, 48)
            for h in range(2):
                n = P if h == 0 else GROUPS - P
                nc.vector.tensor_reduce(lo[0:n, h:h + 1], dst_by_group[0:n, h, :], AX.X, ALU.min).then_inc(start_step, 1)
                nc.vector.tensor_reduce(hi[0:n, h:h + 1], dst_by_group[0:n, h, :], AX.X, ALU.max).then_inc(start_step, 1)
            dve.wait_ge(start_step, 6)
            nc.vector.tensor_tensor(span[:, :], hi[:, :], lo[:, :], ALU.subtract).then_inc(start_step, 1)
            dve.wait_ge(start_step, 7)
            dve.wait_ge(consts_ready, 5)
            for h in range(2):
                nc.vector.tensor_scalar(diag[:, h, :], ident[:, :], lo[:, h:h + 1], None, ALU.mult).then_inc(diag_ready, 1)
                nc.vector.tensor_scalar(diag[:, 2 + h, :], ident[:, :], span[:, h:h + 1], None, ALU.mult).then_inc(diag_ready, 1)
            nc.vector.tensor_copy(type_iota, type_iota_sb[:, :])
            nc.vector.tensor_copy(win_iota, win_iota_sb[:, :]).then_inc(start_step, 1)
            dve.wait_ge(bases_spread, 1)
            nc.vector.tensor_reduce(max_span[:, :], node_ps[:, 256:256 + GROUPS], AX.X, ALU.max).then_inc(start_step, 1)
            dve.wait_ge(start_step, 9)
            nc.vector.tensor_scalar(further[:, :], win_steps[:, :], max_span[:, 0:1], None, ALU.is_le).then_inc(start_step, 1)
            dve.wait_ge(start_step, 10)
            nc.vector.tensor_reduce(n_further[:, :], further[:, :], AX.X, ALU.add).then_inc(start_step, 1)
            dve.wait_ge(start_step, 11)
            nc.vector.tensor_scalar(n_passes[0:1, :], n_further[0:1, :], 1.0, None, ALU.add).then_inc(passes_ready, 1)
            nc.vector.tensor_copy(first_base[:, :], node_ps[:, 0:GROUPS]).then_inc(start_step, 1)
            nc.vector.memset(acc0[0:D, :, :], 0.0)
            nc.vector.memset(acc0[D:D + 1, 0, :], 1.0)
            dve.wait_ge(edges_ready, 4 * -(-BLOCKS // TURN))
            nc.vector.memset(x1_nodes[:, :, D:D + 1], 1.0).then_inc(start_step, 1)
            dve.wait_ge(start_step, 13)
            dve.wait_ge(passes_ready, 1)
            passes = dve.value_load(n_passes[0:1, 0:1], min_val=1, max_val=EXTRA + 1)

            def weigh(layer, step, g, s, chunks, count):
                dve.wait_ge(group_summed, step + 1)
                cols = bass.ds(g * CH, chunks)
                if layer == 0:
                    nc.vector.tensor_tensor(type_hot[:, s, 0:chunks, :],
                                            edges[:, TYPE, cols].unsqueeze(2).to_broadcast([P, chunks, R]),
                                            type_iota.unsqueeze(1).to_broadcast([P, chunks, R]),
                                            ALU.is_equal).then_inc(types_hot, count)
                dve.wait_ge(factors_ready, step + 1)
                nc.vector.tensor_tensor(hits[:, 0:chunks, :], win_iota.unsqueeze(1).to_broadcast([P, chunks, WIN]),
                                        local_dst[:, cols].unsqueeze(2).to_broadcast([P, chunks, WIN]),
                                        ALU.is_equal).then_inc(hits_ready, count)
                if layer == 0:
                    dve.wait_ge(coefs_ready, step + 1)
                    nc.vector.tensor_tensor(coef_w[:, s, 0:chunks, :],
                                            coefs_ps[:, 0:chunks * B].rearrange("p (c b) -> p c b", b=B),
                                            edges[:, WEIGHT, cols].unsqueeze(2).to_broadcast([P, chunks, B]),
                                            ALU.mult).then_inc(coefs_weighted, count)
                    dve.wait_ge(coefs_weighted, step + 2)
                    dve.wait_ge(hits_ready, step + 1)
                    nc.vector.tensor_tensor(factors[:, s, 0:chunks, :, :],
                                            hits[:, 0:chunks, :].unsqueeze(2).to_broadcast([P, chunks, B, WIN]),
                                            coef_w[:, s, 0:chunks, :].unsqueeze(3).to_broadcast([P, chunks, B, WIN]),
                                            ALU.mult).then_inc(factors_ready, count)
                else:
                    dve.wait_ge(hits_ready, step + 1)
                    nc.vector.tensor_tensor(factors[:, s, 0:chunks, 0, :], hits[:, 0:chunks, :],
                                            edges[:, WEIGHT, cols].unsqueeze(2).to_broadcast([P, chunks, WIN]),
                                            ALU.mult).then_inc(factors_ready, count)

            def add_window(layer, step, g, s, count):
                node = dve.value_load(base_int[0:1, bass.ds(g, 1)], min_val=0, max_val=N)
                dve.wait_ge(group_summed, step + 1 + FREE)
                dve.wait_ge(window_added, step + FREE)
                if layer == 0:
                    nc.vector.tensor_tensor(acc0[0:D, :, bass.ds(node, WIN)], acc0[0:D, :, bass.ds(node, WIN)],
                                            sums_ps[s][0:D, 0:B * WIN].rearrange("p (b w) -> p b w", b=B),
                                            ALU.add).then_inc(window_added, count)
                else:
                    nc.vector.tensor_tensor(acc1[:, bass.ds(node, WIN)], acc1[:, bass.ds(node, WIN)],
                                            sums_ps[s][0:D + 1, 0:WIN], ALU.add).then_inc(window_added, count)

            for layer in range(2):
                whole = (GROUPS - 1) * CH
                nc.vector.tensor_copy(base[:, :], first_base[0:1, :]).then_inc(base_ready, 1)
                nc.vector.tensor_copy(base_int[:, :], first_base[0:1, :]).then_inc(base_ready, 1)
                nc.vector.tensor_tensor(local_dst[:, 0:whole].rearrange("p (g c) -> p g c", c=CH),
                                        edges[:, DST, 0:whole].rearrange("p (g c) -> p g c", c=CH),
                                        first_base[:, 0:GROUPS - 1].unsqueeze(2).to_broadcast([P, GROUPS - 1, CH]),
                                        ALU.subtract).then_inc(base_ready, 1)
                nc.vector.tensor_tensor(local_dst[:, whole:CHUNKS], edges[:, DST, whole:CHUNKS],
                                        first_base[:, GROUPS - 1:GROUPS].to_broadcast([P, TAIL]),
                                        ALU.subtract).then_inc(base_ready, 1)
                with dve.Fori(0, passes) as k:
                    kk = k + passes if layer else k
                    step0 = kk * STEPS
                    dve.wait_ge(base_ready, kk * 3 + 4 + 4 * layer)

                    def front(i, s, chunks, count):
                        weigh(layer, step0 + i * U + s, i * U + s, s, chunks, count)

                    def back(i, s, count):
                        add_window(layer, step0 + i * U + s, i * U + s, s, count)

                    front(0, 0, CH, 1)
                    front(0, 1, CH, 1)
                    front(0, 2, CH, 1)
                    if layer:
                        dve.wait_ge(self_added, -(-TILES // 4))
                    back(0, 0, 1)
                    with dve.Fori(1, ITERS) as i:
                        for s in range(U):
                            front(i, s, CH, 1)
                            if s < 2:
                                back(i - 1, s + 1, 1)
                            else:
                                back(i, 0, 1)
                    front(ITERS, 0, TAIL, U)
                    back(ITERS - 1, 1, 1)
                    back(ITERS - 1, 2, 1)
                    back(ITERS, 0, U)
                    dve.wait_ge(window_added, step0 + STEPS + FREE)
                    nc.vector.tensor_scalar(base[:, :], base[:, :], float(WIN), float(N), ALU.add, ALU.min).then_inc(base_ready, 1)
                    nc.vector.tensor_scalar(local_dst[:, :], local_dst[:, :], float(WIN), None, ALU.subtract).then_inc(base_ready, 1)
                    dve.wait_ge(base_ready, kk * 3 + 6 + 4 * layer)
                    nc.vector.tensor_copy(base_int[:, :], base[:, :]).then_inc(base_ready, 1)

                if layer == 0:
                    dve.wait_ge(x_loaded, 32)
                for b in range(BATCHES):
                    turns = BATCHES * layer + b
                    dve.wait_ge(nodes_out, turns + 1)
                    bank = sums_ps[b % 2]
                    tiles = slice(b * BATCH, (b + 1) * BATCH)
                    done = 3 * BATCHES + 7 * b if layer else 3 * b
                    if layer == 0:
                        nc.vector.scalar_tensor_tensor(h_nodes[:, :, :], bank[:, 0:BATCH * D].rearrange("p (t f) -> p t f", t=BATCH),
                                                       0.0, x_nodes[:, tiles, :], ALU.max, ALU.add).then_inc(nodes_read, 1)
                    else:
                        rows = bank[:, 0:BATCH * (D + 1)].rearrange("p (t f) -> p t f", t=BATCH)
                        nc.vector.tensor_scalar(has_deg[:, :], rows[:, :, D], 0.0, None, ALU.is_gt).then_inc(norm_step, 1)
                        nc.vector.tensor_scalar(safe_deg[:, :], rows[:, :, D], TINY, None, ALU.max).then_inc(norm_step, 1)
                        dve.wait_ge(norm_step, done + 2)
                        nc.vector.reciprocal(inv_deg[:, :], safe_deg[:, :]).then_inc(norm_step, 1)
                        dve.wait_ge(norm_step, done + 3)
                        nc.vector.tensor_tensor(inv_deg[:, :], inv_deg[:, :], has_deg[:, :], ALU.mult).then_inc(norm_step, 1)
                        dve.wait_ge(norm_step, done + 4)
                        done += 4
                        for t in range(BATCH):
                            last = nc.vector.scalar_tensor_tensor(h_nodes[:, t, :], rows[:, t, 0:D], inv_deg[:, t:t + 1],
                                                                  x_nodes[:, b * BATCH + t, :], ALU.mult, ALU.add)
                        last.then_inc(nodes_read, 1)
                    dve.wait_ge(nodes_read, turns + 1)
                    for t in range(BATCH):
                        last = nc.vector.bn_stats(stats[:, t, :], h_nodes[:, t, :])
                    last.then_inc(norm_step, 1)
                    dve.wait_ge(norm_step, done + 1)
                    for t in range(BATCH):
                        last = nc.vector.bn_aggr(mean_var[:, t, :], stats[:, t, :])
                    last.then_inc(norm_step, 1)
                    dve.wait_ge(norm_step, done + 2)
                    nc.vector.tensor_scalar(var_eps[:, :], mean_var[:, :, 1], EPS, None, ALU.add).then_inc(var_ready, 1)
                    dve.wait_ge(std_ready, turns + 1)
                    nc.vector.reciprocal(rstd[:, :], std[:, :]).then_inc(norm_step, 1)
                    dve.wait_ge(norm_step, done + 3)
                    to = x1_nodes if layer == 0 else y_nodes
                    for t in range(BATCH):
                        last = nc.vector.tensor_scalar(to[:, b * BATCH + t, 0:D], h_nodes[:, t, :], mean_var[:, t, 0:1],
                                                       rstd[:, t:t + 1], ALU.subtract, ALU.mult)
                    last.then_inc(x1_ready if layer == 0 else y_ready, 1)
                    dve.wait_ge(x1_ready if layer == 0 else y_ready, b + 1)
                if layer == 0:
                    for q in range(-(-TILES // 4)):
                        n = min(4, TILES - 4 * q) * P
                        dve.wait_ge(x1_turned, q + 1)
                        nc.vector.tensor_copy(acc1[:, q * 4 * P:q * 4 * P + n], node_ps[0:D + 1, 0:n]).then_inc(self_added, 1)
                    dve.wait_ge(params_loaded, 16 * N_PARAMS)
                    nc.vector.tensor_tensor(x_nodes[:, :, :], x1_nodes[:, :, 0:D],
                                            bias1_bc[:, :].unsqueeze(1).to_broadcast([P, TILES, D]), ALU.add).then_inc(bias_added, 1)
                    dve.wait_ge(bias_added, 1)


_INS = ['x', 'src', 'dst', 'edge_type_32', 'edge_weight', 'L0_gnn_weight', 'L0_gnn_w_comp', 'L0_gnn_bias', 'L1_gnn_W', 'L1_gnn_b']
_FILL = {'src': 0, 'dst': N - 1, 'edge_type_32': 0, 'edge_weight': 0}


def kernel(**inputs):
    import numpy as _np
    import concourse.bacc as _bacc
    from concourse import mybir as _mybir
    from concourse.bass_utils import run_bass_kernel_spmd as _run

    nc = _bacc.Bacc("TRN2", target_bir_lowering=False, num_devices=1)
    arrays, args = {}, []
    for name in _INS:
        a = _np.ascontiguousarray(inputs[name])
        if name in _FILL:
            a = _np.concatenate([a, _np.full((CHUNKS * P - E,), _FILL[name], a.dtype)])
        arrays[f"in_{name}"] = a
        args.append(nc.dram_tensor(f"in_{name}", a.shape, _mybir.dt.from_np(a.dtype), kind="ExternalInput").ap())
    y = nc.dram_tensor("out_y", (N, D), _mybir.dt.float32, kind="ExternalOutput").ap()
    gnn_two_layers(nc, *args, y)
    r = _run(nc, [arrays], core_ids=[0])
    return r.results[0]["out_y"]
```

```python
import concourse.bass as bass
from concourse import mybir
from contextlib import ExitStack


N = 6250
E = 200000
D = 64
R = 32
B = 4
P = 128
CH = 8
U = 3
WIN = 44
CHUNKS = -(-E // P)
ITERS = CHUNKS // (CH * U)
TAIL = CHUNKS - ITERS * CH * U
GROUPS = ITERS * U + 1
BLOCKS = -(-CHUNKS // P)
LEFT = CHUNKS - (BLOCKS - 1) * P
TURN = 4
TURNS = -(-BLOCKS // TURN)
STEPS = (ITERS + 1) * U
TILES = -(-N // P)
NPAD = TILES * P + max(WIN, 72)
BATCH = 7
BATCHES = TILES // BATCH
HALF = B // 2
PARTS = [(0, 3), (3, BATCHES)]
EXTRA = -(-N // WIN)
DENSE = 16
DENSE_CHUNKS = ITERS * DENSE
SPREAD = 7
WB = 72
LEAST = 60
BLK = TILES * WB
KEYS = TILES * SPREAD
DENSE_OF = [range(0, 6), range(6, 10), range(10, 16)]
PAIRS = DENSE // 2
BLOCKS_OF = [(ITERS + 1) // 2, ITERS // 2]
ROUND = 12582912.0
FAST = ITERS + 1
SPAN6 = 6
EPS = 1e-5
TINY = 1.1754943508222875e-38
assert 0 < TAIL <= CH and TILES == BATCH * BATCHES and GROUPS <= 2 * P
assert CH * U > DENSE and (ITERS - 1) % 2 == 0 and FAST % SPAN6 == 0 and WB <= NPAD - TILES * P <= 2 * BLK
LAST = N - (TILES - 1) * P


def gnn_two_layers(nc, x, src, dst, etype, eweight, w0, w_comp, bias0, w1, bias1, out):
    f32 = mybir.dt.float32
    i32 = mybir.dt.int32
    bf16 = mybir.dt.bfloat16
    f16 = mybir.dt.float16
    ALU = mybir.AluOpType
    ACT = mybir.ActivationFunctionType
    AX = mybir.AxisListType

    table = nc.dram_tensor("x1_table", (TILES * P, D), f32, kind="Internal").ap()
    block_table = nc.dram_tensor("block_table", (ITERS * P, BLK), f32, kind="Internal").ap()
    edge_arrays = (src, dst, etype, eweight)
    SRC, DST, TYPE, WEIGHT = range(4)

    ctx = ExitStack()
    with ctx:
        def sb(name, shape, dt=f32):
            return ctx.enter_context(nc.sbuf_tensor(name, shape, dt))

        def pb(name, shape):
            return ctx.enter_context(nc.psum_tensor(name, shape, f32))

        def sem(name):
            return ctx.enter_context(nc.semaphore(name))

        ident = sb("ident", [P, P])
        ones = sb("ones", [P, P])
        type_iota_sb = sb("type_iota_sb", [P, R])
        win_iota_sb = sb("win_iota_sb", [P, WIN])
        win_steps = sb("win_steps", [P, EXTRA])
        lo = sb("lo", [P, 2])
        hi = sb("hi", [P, 2])
        span = sb("span", [P, 2])
        first_base = sb("first_base", [P, GROUPS])
        base = sb("base", [1, GROUPS])
        base_int = sb("base_int", [1, GROUPS], i32)
        max_span = sb("max_span", [P, 1])
        further = sb("further", [P, EXTRA])
        n_further = sb("n_further", [P, 1])
        n_passes = sb("n_passes", [1, 1], i32)
        edges = sb("edges", [P, 4, CHUNKS])
        local_dst = sb("local_dst", [P, CHUNKS])
        idx = sb("idx", [P, U, CH], i32)
        gathered_rows = sb("gathered_rows", [P, U, CH, D + 16])
        type_hot = sb("type_hot", [P, U, CH, R])
        type_hot_t = sb("type_hot_t", [P, 2, P])
        coef_w = sb("coef_w", [P, U, CH, B])
        factors_room = sb("factors_room", [P, U * CH * B * WIN])
        factors = factors_room[:, :].rearrange("p (s c b w) -> p s c b w", s=U, c=CH, b=B)
        dst_by_group = factors_room[:, 0:2 * P * CH].bitcast(i32).rearrange("p (h e) -> p h e", h=2)
        starts = sb("starts", [P, ITERS, DENSE])
        offsets = sb("offsets", [1, ITERS, DENSE], i32)
        hi_key = sb("hi_key", [P, ITERS, DENSE], f16)
        lo_key = sb("lo_key", [P, ITERS, DENSE], f16)
        node_key = sb("node_key", [P, ITERS, DENSE], f16)
        w_part = [sb(f"w_part{w}", [P, ITERS, DENSE], bf16) for w in range(3)]
        key_iota = sb("key_iota", [P, KEYS, 2], f16)
        key_iota_f = factors_room[:, 2 * P * CH:2 * P * CH + 2 * KEYS].rearrange("p (v t) -> p v t", t=2)
        diag = factors_room[:, 3 * P * CH:3 * P * CH + 4 * P].rearrange("p (d e) -> p d e", d=4)
        lo_room = sb("lo_room", [P, 3 * PAIRS * P])
        node_room = sb("node_room", [P, PAIRS * KEYS])
        lo_hot = lo_room[:, :].bitcast(bf16).rearrange("p (w q e t) -> p w q e t", w=3, q=PAIRS, t=2)
        node_hot = node_room[:, :].bitcast(bf16).rearrange("p (q v t) -> p q v t", q=PAIRS, t=2)
        carry_hot = sb("carry_hot", [P, PAIRS, TILES, 2], bf16)
        hi_part = lo_room[:, 0:DENSE_CHUNKS].rearrange("p (i j) -> p i j", j=DENSE)
        spare = lo_room[:, DENSE_CHUNKS:2 * DENSE_CHUNKS].rearrange("p (i j) -> p i j", j=DENSE)
        place = node_room[:, 0:DENSE_CHUNKS].rearrange("p (i j) -> p i j", j=DENSE)
        greatest = sb("greatest", [P, 3, 2])
        least = sb("least", [P, 4, 2])
        broken = sb("broken", [P, 7, 2])
        n_broken = sb("n_broken", [P, 1])
        not_fast = sb("not_fast", [1, 1])
        loops = sb("loops", [1, 2], i32)
        zero = sb("zero", [P, 1])
        wc_blocks = sb("wc_blocks", [P, 4 * B])
        w0_sb = sb("w0_sb", [P, HALF, D])
        w1_sb = sb("w1_sb", [D + 1, D])
        deg_col = sb("deg_col", [D + 1, 1])
        bias0_bc = sb("bias0_bc", [P, D])
        neg_bias0 = sb("neg_bias0", [P, D])
        bias1_bc = sb("bias1_bc", [P, D])
        x_nodes = sb("x_nodes", [P, TILES, D])
        room = sb("room", [P, 2 * BLK])
        edge_rows = room[:, 0:4 * BLOCKS * P].rearrange("p (a t e) -> p a t e", a=4, t=BLOCKS)
        blocks_out = room[:, :].rearrange("p (b h w) -> p b h w", b=2, h=TILES)
        x1_nodes = room[:, 0:TILES * (D + 1)].rearrange("p (t f) -> p t f", f=D + 1)
        h_nodes = room[:, TILES * (D + 1):TILES * (2 * D + 1)].rearrange("p (t f) -> p t f", f=D)
        acc_room = sb("acc_room", [P, NPAD + 2 * BLK])
        acc0 = acc_room[:, 0:HALF * NPAD].rearrange("p (b n) -> p b n", b=HALF)
        acc1 = acc_room[0:D + 1, 0:NPAD]
        blocks_in = acc_room[:, NPAD:NPAD + 2 * BLK].rearrange("p (b h w) -> p b h w", b=2, h=TILES)
        stats = sb("stats", [P, TILES, 6])
        mean = sb("mean", [P, TILES])
        half_diff = sb("half_diff", [P, TILES])
        var_eps = sb("var_eps", [P, TILES])
        std = sb("std", [P, TILES])
        rstd = sb("rstd", [P, TILES])
        newton = sb("newton", [P, TILES])
        neg_mean_rstd = sb("neg_mean_rstd", [P, TILES])
        has_deg = sb("has_deg", [P, TILES])
        inv_deg = sb("inv_deg", [P, TILES])

        types_ps = pb("types_ps", [P, 512])
        coefs_ps = pb("coefs_ps", [P, 512])
        turn_ps = [types_ps, coefs_ps]
        dve_ps = pb("dve_ps", [P, 512])
        type_iota = dve_ps[:, 0:R]
        win_iota = dve_ps[:, R:R + WIN]
        hits = dve_ps[:, 128:128 + CH * WIN].rearrange("p (c w) -> p c w", c=CH)
        sums_ps = [pb(f"sums_ps{s}", [P, 512]) for s in range(U)]
        node_ps = pb("node_ps", [P, 512])
        dense_ps = [pb("dense_ps", [P, 512]), node_ps]

        x_loaded = sem("x_loaded")
        params_loaded = sem("params_loaded")
        dst_loaded = sem("dst_loaded")
        consts_ready = sem("consts_ready")
        pool_step = sem("pool_step")
        params_zeroed = sem("params_zeroed")
        diag_ready = sem("diag_ready")
        bases_spread = sem("bases_spread")
        passes_ready = sem("passes_ready")
        start_step = sem("start_step")
        base_ready = sem("base_ready")
        rows_loaded = [sem(f"rows_loaded{a}") for a in range(4)]
        rows_are_float = [sem(f"rows_are_float{a}") for a in range(3)]
        sources_ready = sem("sources_ready")
        acc_zeroed = sem("acc_zeroed")
        rows_turned = sem("rows_turned")
        edges_ready = sem("edges_ready")
        idx_ready = sem("idx_ready")
        gathers_begun = sem("gathers_begun")
        rows_gathered = [sem(f"rows_gathered{s}") for s in range(U)]
        types_hot = sem("types_hot")
        types_turned = sem("types_turned")
        types_copied = sem("types_copied")
        coefs_ready = sem("coefs_ready")
        dst_local = sem("dst_local")
        hits_ready = sem("hits_ready")
        coefs_weighted = sem("coefs_weighted")
        factors_ready = sem("factors_ready")
        group_summed = sem("group_summed")
        window_added = sem("window_added")
        nodes_out = sem("nodes_out")
        nodes_read = sem("nodes_read")
        nodes_added = sem("nodes_added")
        degs_out = sem("degs_out")
        deg_step = sem("deg_step")
        stats_ready = sem("stats_ready")
        norm_step = sem("norm_step")
        var_ready = sem("var_ready")
        std_ready = sem("std_ready")
        norm_ready = sem("norm_ready")
        bias_ready = sem("bias_ready")
        bias_added = sem("bias_added")
        part_a_normed = sem("part_a_normed")
        part_b_normed = sem("part_b_normed")
        x1_turned = sem("x1_turned")
        self_added = sem("self_added")
        x1_stored = sem("x1_stored")
        starts_spread = sem("starts_spread")
        starts_ready = sem("starts_ready")
        key_step = sem("key_step")
        lo_hots_ready = sem("lo_hots_ready")
        hots_ready = sem("hots_ready")
        dense_summed = sem("dense_summed")
        chunk_copied = sem("chunk_copied")
        tail_zeroed = sem("tail_zeroed")
        blocks_stored = [sem(f"blocks_stored{r}") for r in range(2)]
        checked = sem("checked")
        broken_counted = sem("broken_counted")
        loop_step = sem("loop_step")
        loops_ready = sem("loops_ready")
        block_loaded = [sem(f"block_loaded{r}") for r in range(2)]
        block_summed = sem("block_summed")
        block_added = sem("block_added")
        y_stored = sem("y_stored")

        block = ctx.enter_context(nc.Block())

        N_PARAMS = 4 + 2 + 1 + 2
        WHOLE = 16 * CH
        PER_PASS = [ITERS * WHOLE + (16 * TAIL if s == 0 else 0) for s in range(U)]
        FREE = 2 * U + 1
        FREE_BANKS = 2
        FREE_HOTS = DENSE

        def chunks_of(g):
            return TAIL if g == GROUPS - 1 else CH

        def weight_of(tail):
            return U if tail else 1

        def slot_is_free(step, count):
            return step + FREE - (U - 1) * count

        def load_loops(engine):
            engine.wait_ge(loops_ready, 1)
            return (engine.value_load(loops[0:1, 0:1], min_val=0, max_val=EXTRA + 1),
                    engine.value_load(loops[0:1, 1:2], min_val=0, max_val=1))

        KEY_STEPS = 22
        START_BANKS = [(i0, min(i0 + 512 // DENSE, ITERS)) for i0 in range(0, ITERS, 512 // DENSE)]

        def load_rows(queue, a):
            to = edge_rows[:, a, :, :] if a == WEIGHT else edge_rows[:, a, :, :].bitcast(i32)
            rows = edge_arrays[a].rearrange("(c e) -> c e", e=P)
            whole = (BLOCKS - 1) * P
            queue.dma_start(to[:, 0:BLOCKS - 1, :], rows[0:whole, :].rearrange("(t p) e -> p t e", p=P)).then_inc(rows_loaded[a], 16)
            queue.dma_start(to[0:LEFT, BLOCKS - 1, :], rows[whole:CHUNKS, :]).then_inc(rows_loaded[a], 16)

        @block.sync
        def _(sp):
            sp.dma_start(dst_by_group[:, 0, :], dst[0:P * P * CH].rearrange("(g e) -> g e", g=P)).then_inc(dst_loaded, 16)
            rest = GROUPS - 1 - P
            sp.dma_start(dst_by_group[0:rest, 1, :],
                         dst[P * P * CH:(GROUPS - 1) * P * CH].rearrange("(g e) -> g e", g=rest)).then_inc(dst_loaded, 16)
            sp.dma_start(dst_by_group[rest:rest + 1, 1, :],
                         dst[(CHUNKS - CH) * P:CHUNKS * P].rearrange("(g e) -> g e", g=1)).then_inc(dst_loaded, 16)
            for a in (DST, TYPE, WEIGHT):
                load_rows(sp, a)
            sp.wait_ge(params_zeroed, 1)
            for j in range(4):
                sp.dma_start(wc_blocks[R * j:R * j + R, B * j:B * j + B], w_comp[:, :]).then_inc(params_loaded, 16)
            for h in range(2):
                sp.dma_start(w0_sb[D * h:D * h + D, :, :], w0[HALF * h:HALF * h + HALF].rearrange("b i o -> i b o")).then_inc(params_loaded, 16)
            sp.dma_start(w1_sb[0:D, :], w1[:, :]).then_inc(params_loaded, 16)
            sp.dma_start(bias0_bc[:, :], bias0.rearrange("(a o) -> a o", a=1).to_broadcast([P, D])).then_inc(params_loaded, 16)
            sp.dma_start(bias1_bc[:, :], bias1.rearrange("(a o) -> a o", a=1).to_broadcast([P, D])).then_inc(params_loaded, 16)
            sp.dma_start(x_nodes[:, 0:TILES - 1, :], x[0:(TILES - 1) * P, :].rearrange("(t p) f -> p t f", p=P)).then_inc(x_loaded, 16)
            sp.dma_start(x_nodes[0:LAST, TILES - 1, :], x[(TILES - 1) * P:N, :]).then_inc(x_loaded, 16)
            for r in range(2):
                sp.sem_inc(blocks_stored[r], 16)
            sp.wait_ge(passes_ready, 1)
            passes = sp.value_load(n_passes[0:1, 0:1], min_val=1, max_val=EXTRA + 1)

            def store_block(k, b, r):
                sp.wait_ge(chunk_copied, (k * ITERS + b) * DENSE + DENSE + FREE_BANKS)
                sp.dma_start(block_table[bass.ds(b * P, P), :], blocks_out[:, r, :, :].rearrange("p h w -> p (h w)")).then_inc(blocks_stored[r], 16)

            with sp.Fori(0, passes) as k:
                with sp.Fori(0, ITERS // 2) as m:
                    for r in range(2):
                        store_block(k, m * 2 + r, r)
                store_block(k, ITERS - 1, 0)
            for done, (b0, b1) in zip((part_a_normed, part_b_normed), PARTS):
                sp.wait_ge(done, 1)
                sp.dma_start(table[b0 * BATCH * P:b1 * BATCH * P, :].rearrange("(t p) f -> p t f", p=P),
                             x1_nodes[:, b0 * BATCH:b1 * BATCH, 0:D]).then_inc(x1_stored, 16)
            slow, fast = load_loops(sp)
            sp.wait_ge(nodes_out, BATCHES)

            def load_block(f, r):
                sp.wait_ge(block_summed, f + 1)
                sp.dma_start(blocks_in[:, r, :, :].rearrange("p h w -> p (h w)"), block_table[bass.ds(f * P, P), :]).then_inc(block_loaded[r], 16)

            with sp.If(fast == 1):
                with sp.Fori(0, FAST // SPAN6 - 1) as m:
                    for q in range(SPAN6):
                        load_block(m * SPAN6 + q, q % 2)
                for f in range(FAST - SPAN6, ITERS):
                    load_block(f, f % 2)
            for done, (b0, b1) in zip((part_a_normed, part_b_normed), PARTS):
                sp.wait_ge(done, 2)
                t0, t1 = b0 * BATCH, min(b1 * BATCH, TILES - 1)
                sp.dma_start(out[t0 * P:t1 * P, :].rearrange("(t p) f -> p t f", p=P),
                             h_nodes[:, t0:t1, :]).then_inc(y_stored, 16)
            sp.dma_start(out[(TILES - 1) * P:N, :], h_nodes[0:LAST, TILES - 1, :]).then_inc(y_stored, 16)
            sp.wait_ge(y_stored, 16 * (len(PARTS) + 1))

        @block.gpsimd
        def _(pool):
            nc.gpsimd.memset(ones[:, :], 1.0).then_inc(pool_step, 1)
            nc.gpsimd.memset(ident[:, :], 0.0).then_inc(pool_step, 1)
            pool.wait_ge(pool_step, 2)
            nc.gpsimd.affine_select(out=ident[:, :], in_=ident[:, :], compare_op=ALU.not_equal, fill=1.0, base=0,
                                    pattern=[[-1, P]], channel_multiplier=1).then_inc(consts_ready, 1)
            nc.gpsimd.iota(type_iota_sb[:, :], pattern=[[1, R]], base=0, channel_multiplier=0,
                           allow_small_or_imprecise_dtypes=True).then_inc(consts_ready, 1)
            nc.gpsimd.iota(win_iota_sb[:, :], pattern=[[1, WIN]], base=0, channel_multiplier=0,
                           allow_small_or_imprecise_dtypes=True).then_inc(consts_ready, 1)
            nc.gpsimd.iota(win_steps[:, :], pattern=[[WIN, EXTRA]], base=WIN, channel_multiplier=0,
                           allow_small_or_imprecise_dtypes=True).then_inc(consts_ready, 1)
            nc.gpsimd.memset(gathered_rows[:, :, :, D:D + 1], 1.0).then_inc(consts_ready, 1)
            nc.gpsimd.iota(key_iota_f, pattern=[[1, KEYS], [0, 2]], base=0, channel_multiplier=0,
                           allow_small_or_imprecise_dtypes=True).then_inc(consts_ready, 1)
            nc.gpsimd.memset(acc0[:, :, :], 0.0).then_inc(acc_zeroed, 1)
            pool.wait_ge(passes_ready, 1)
            passes = pool.value_load(n_passes[0:1, 0:1], min_val=1, max_val=EXTRA + 1)

            def gather_group(step, s, chunks, rows):
                pool.wait_ge(idx_ready, step + 1)
                pool.sem_inc(gathers_begun, 1)
                for j in range(chunks):
                    pool.indirect_dma_start(gathered_rows[:, s, j, 0:D], None, rows,
                                            bass.IndirectOffsetOnAxis(ap=idx[:, s, j:j + 1], axis=0)
                                            ).then_inc(rows_gathered[s], 16)

            def gather_all(layer, k):
                step0 = (k + passes if layer else k) * STEPS
                rows = table[:, :] if layer else x[:, :]
                with pool.Fori(0, ITERS) as i:
                    for s in range(U):
                        gather_group(step0 + i * U + s, s, CH, rows)
                gather_group(step0 + ITERS * U, 0, TAIL, rows)

            with pool.Fori(0, passes) as k:
                gather_all(0, k)
            pool.wait_ge(x_loaded, 32)
            pool.wait_ge(params_loaded, 16 * N_PARAMS)
            nc.gpsimd.tensor_tensor(x_nodes[:, :, :], x_nodes[:, :, :], bias0_bc[:, :].unsqueeze(1).to_broadcast([P, TILES, D]),
                                    ALU.add).then_inc(bias_added, 1)
            slow, fast = load_loops(pool)
            pool.wait_ge(x1_stored, 16 * len(PARTS))
            with pool.If(fast == 0), pool.Fori(0, slow) as k:
                gather_all(1, k)
            with pool.If(fast == 1):
                with pool.Fori(0, FAST // SPAN6 - 1) as m:
                    for q in range(SPAN6):
                        gather_group((passes * ITERS + passes + m * SPAN6 + q) * U, q % U, CH, table[:, :])
                for f in range(FAST - SPAN6, FAST):
                    gather_group((passes * ITERS + passes + f) * U, f % U, TAIL if f == ITERS else CH, table[:, :])
            pool.wait_ge(part_a_normed, 1)
            pool.wait_ge(part_b_normed, 1)
            pool.wait_ge(nodes_added, BATCHES)
            nc.gpsimd.tensor_tensor(x_nodes[:, :, :], x1_nodes[:, :, 0:D], bias1_bc[:, :].unsqueeze(1).to_broadcast([P, TILES, D]),
                                    ALU.add).then_inc(bias_added, 1)

        @block.scalar
        def _(act):
            load_rows(act, SRC)
            act.wait_ge(rows_loaded[SRC], 32)
            rows = edge_rows[:, SRC, :, :]
            nc.scalar.copy(rows[:, 0:BLOCKS - 1, :], rows[:, 0:BLOCKS - 1, :].bitcast(i32)).then_inc(rows_are_float[SRC], 1)
            nc.scalar.copy(rows[0:LEFT, BLOCKS - 1, :], rows[0:LEFT, BLOCKS - 1, :].bitcast(i32)).then_inc(rows_are_float[SRC], 1)
            for m, t in enumerate(range(0, BLOCKS, TURN)):
                n = min(TURN * P, CHUNKS - t * P)
                act.wait_ge(rows_turned, m + 1)
                nc.scalar.copy(edges[:, SRC, t * P:t * P + n], turn_ps[m % 2][:, 0:n]).then_inc(sources_ready, 1)
            act.wait_ge(sources_ready, TURNS)
            act.wait_ge(passes_ready, 1)
            passes = act.value_load(n_passes[0:1, 0:1], min_val=1, max_val=EXTRA + 1)

            def index_group(layer, step, g, s, chunks, count, unit=1):
                act.wait_ge(group_summed, slot_is_free(step, unit))
                nc.scalar.copy(idx[:, s, 0:chunks], edges[:, SRC, bass.ds(g * CH, chunks)]).then_inc(idx_ready, count)
                if layer == 0:
                    act.wait_ge(types_turned, step + 1)
                    for h in range(-(-chunks // 4)):
                        n = min(4, chunks - 4 * h) * R
                        last = nc.scalar.copy(type_hot_t[0:n, h, :], types_ps[0:n, h * P:h * P + P])
                    last.then_inc(types_copied, count)

            def norm_part(layer, part):
                b0, b1 = PARTS[part]
                tiles = slice(b0 * BATCH, b1 * BATCH)
                act.wait_ge(var_ready, 2 * layer + part + 1)
                nc.scalar.activation(std[:, tiles], var_eps[:, tiles], ACT.Sqrt).then_inc(std_ready, 1)
                if part == 0:
                    act.wait_ge(norm_ready, layer + 1)
                    to = h_nodes if layer else x1_nodes
                    for t in range(b0 * BATCH, b1 * BATCH):
                        last = nc.scalar.activation(to[:, t, 0:D], h_nodes[:, t, :], ACT.Identity,
                                                    scale=rstd[:, t:t + 1], bias=neg_mean_rstd[:, t:t + 1])
                    last.then_inc(part_a_normed, 1)

            def begin_block(k, b, r, use):
                act.wait_ge(blocks_stored[r], (k * BLOCKS_OF[r] + use) * 16 + 16)
                nc.scalar.copy(blocks_out[:, r, :, LEAST:WB], zero[:, 0:1].unsqueeze(2).to_broadcast([P, TILES, WB - LEAST])).then_inc(tail_zeroed, 1)

            def copy_chunk(k, b, r, j):
                n = (k * ITERS + b) * DENSE + j
                offset = act.value_load(offsets[0:1, bass.ds(b, 1), j:j + 1].rearrange("p i j -> p (i j)"), min_val=0, max_val=WB - SPREAD)
                if j == 0:
                    act.wait_ge(tail_zeroed, k * ITERS + b + 1)
                act.wait_ge(dense_summed, n + 1 + FREE_HOTS)
                act.wait_ge(chunk_copied, n + FREE_BANKS)
                nc.scalar.copy(blocks_out[:, r, :, bass.ds(offset, SPREAD)],
                               dense_ps[j % 2][:, 0:KEYS].rearrange("p (h w) -> p h w", h=TILES)).then_inc(chunk_copied, 1)

            act.wait_ge(starts_ready, 4)
            with act.Fori(0, passes) as k:
                step0 = k * STEPS
                for s in range(U):
                    index_group(0, step0 + s, s, s, CH, 1)
                with act.Fori(0, ITERS // 2) as m:
                    for r in range(2):
                        i = m * 2 + (r + 1)
                        for s in range(U):
                            index_group(0, step0 + i * U + s, i * U + s, s, CH, 1)
                            if s == 0:
                                begin_block(k, m * 2 + r, r, m)
                            for j in DENSE_OF[s]:
                                copy_chunk(k, m * 2 + r, r, j)
                index_group(0, step0 + ITERS * U, ITERS * U, 0, TAIL, U)
                begin_block(k, ITERS - 1, 0, ITERS // 2)
                for j in range(DENSE):
                    copy_chunk(k, ITERS - 1, 0, j)
            for part in range(len(PARTS)):
                norm_part(0, part)
            slow, fast = load_loops(act)
            with act.If(fast == 0), act.Fori(0, slow) as k:
                step0 = (k + passes) * STEPS
                with act.Fori(0, ITERS) as i:
                    for s in range(U):
                        index_group(1, step0 + i * U + s, i * U + s, s, CH, 1)
                index_group(1, step0 + ITERS * U, ITERS * U, 0, TAIL, U)
            with act.If(fast == 1):
                step0 = passes * STEPS
                with act.Fori(0, FAST // SPAN6 - 1) as m:
                    for q in range(SPAN6):
                        f = m * SPAN6 + q
                        index_group(1, step0 + f * U, f * U + (U - 1), q % U, CH, U, U)
                for f in range(FAST - SPAN6, ITERS):
                    index_group(1, step0 + f * U, f * U + (U - 1), f % U, CH, U, U)
                index_group(1, step0 + ITERS * U, ITERS * U, ITERS % U, TAIL, U, U)
            for part in range(len(PARTS)):
                norm_part(1, part)

        @block.tensor
        def _(pe):
            pe.sem_inc(group_summed, FREE)
            pe.sem_inc(dense_summed, FREE_HOTS)
            pe.sem_inc(block_summed, FREE_BANKS)
            pe.wait_ge(consts_ready, 6)
            turned = 0
            for a in (SRC, DST, TYPE, WEIGHT):
                if a == WEIGHT:
                    pe.wait_ge(rows_loaded[a], 32)
                else:
                    pe.wait_ge(rows_are_float[a], 2)
                for t0 in range(0, BLOCKS, TURN):
                    if a == SRC and turned >= 2:
                        pe.wait_ge(sources_ready, turned - 1)
                    elif turned > TURNS + 1:
                        pe.wait_ge(edges_ready, turned - TURNS - 1)
                    for t in range(t0, min(t0 + TURN, BLOCKS)):
                        n = min(P, CHUNKS - t * P)
                        last = nc.tensor.transpose(turn_ps[turned % 2][:, (t - t0) * P:(t - t0) * P + n],
                                                   edge_rows[0:n, a, t, :], ident[0:n, 0:n])
                    last.then_inc(rows_turned, 1)
                    turned += 1
                if a == SRC:
                    pe.wait_ge(diag_ready, 4)
                    for h in range(2):
                        n = P if h == 0 else GROUPS - P
                        nc.tensor.matmul(node_ps[:, P * h:P * h + n], ones[:, :], diag[:, h, 0:n], start=True, stop=True)
                        last = nc.tensor.matmul(node_ps[:, 256 + P * h:256 + P * h + n], ones[:, :], diag[:, 2 + h, 0:n],
                                                start=True, stop=True)
                    last.then_inc(bases_spread, 1)
                    pe.wait_ge(sources_ready, TURNS)
            pe.wait_ge(edges_ready, 3 * TURNS)
            for h, (i0, i1) in enumerate(START_BANKS):
                last = nc.tensor.matmul(sums_ps[h][:, 0:(i1 - i0) * DENSE].rearrange("p (i j) -> p i j", j=DENSE),
                                        ident[:, 0:1].to_broadcast([P, P]),
                                        edges[:, DST, i0 * U * CH:i1 * U * CH].rearrange("p (i c) -> p i c", c=U * CH)[:, :, 0:DENSE],
                                        start=True, stop=True)
            last.then_inc(starts_spread, 1)
            pe.wait_ge(starts_ready, 3)
            pe.wait_ge(params_loaded, 16 * N_PARAMS)
            pe.wait_ge(passes_ready, 1)
            passes = pe.value_load(n_passes[0:1, 0:1], min_val=1, max_val=EXTRA + 1)

            def turn_types(step, s, chunks, count):
                pe.wait_ge(types_hot, step + 1)
                for h in range(-(-chunks // 4)):
                    n = min(4, chunks - 4 * h)
                    last = nc.tensor.transpose(types_ps[0:n * R, h * P:h * P + P],
                                               type_hot[:, s, 4 * h:4 * h + n, :].rearrange("p c r -> p (c r)"),
                                               ident[:, :])
                last.then_inc(types_turned, count)

            def look_up_coefs(step, s, chunks, count):
                pe.wait_ge(types_copied, step + 1)
                pe.wait_ge(coefs_weighted, step + 1)
                for h in range(-(-chunks // 4)):
                    n = min(4, chunks - 4 * h)
                    last = nc.tensor.matmul(coefs_ps[:, 4 * h * B:(4 * h + n) * B], type_hot_t[0:n * R, h, :],
                                            wc_blocks[0:n * R, 0:n * B], start=True, stop=True)
                last.then_inc(coefs_ready, count)

            def sum_chunk(k, b, j):
                n = (k * ITERS + b) * DENSE + j
                pe.wait_ge(hots_ready, n + 1)
                if j == 0:
                    pe.wait_ge(chunk_copied, n + 1)
                for w in range(3):
                    last = nc.tensor.matmul(dense_ps[j % 2][:, 0:KEYS], lo_hot[:, w, j // 2, :, j % 2], node_hot[:, j // 2, :, j % 2],
                                            start=(j == 0 and w == 0), stop=(w == 2), skip_group_check=True)
                last.then_inc(dense_summed, 1)
                if j < DENSE - 1:
                    pe.wait_ge(chunk_copied, n + 2)
                    seam = dense_ps[1 - j % 2][:, 0:KEYS].rearrange("p (h w) -> p h w", h=TILES)[:, :, 0]
                    for w in range(3):
                        nc.tensor.matmul(seam, lo_hot[:, w, j // 2, :, j % 2], carry_hot[:, j // 2, :, j % 2],
                                         start=(w == 0), stop=(w == 2), skip_group_check=True)

            def sum_group(layer, step, s, use, chunks, count, unit=1, beside=None):
                pe.wait_ge(rows_gathered[s], use)
                pe.wait_ge(factors_ready, step + 2)
                pe.wait_ge(window_added, slot_is_free(step, unit))
                for j in range(chunks):
                    if layer == 0:
                        for h in range(2):
                            last = nc.tensor.matmul(sums_ps[s][D * h:D * h + D, 0:HALF * WIN], gathered_rows[:, s, j, 0:D],
                                                    factors[:, s, j, HALF * h:HALF * h + HALF, :].rearrange("p b w -> p (b w)"),
                                                    start=(j == 0), stop=(j == chunks - 1))
                    else:
                        last = nc.tensor.matmul(sums_ps[s][0:D + 1, 0:WIN], gathered_rows[:, s, j, 0:D + 1],
                                                factors[:, s, j, 0, :], start=(j == 0), stop=(j == chunks - 1))
                    if j == chunks - 1:
                        last.then_inc(group_summed, count)
                    if beside and j < len(beside[2]):
                        sum_chunk(beside[0], beside[1], beside[2][j])

            def sum_block(f, r, loads):
                pe.wait_ge(block_loaded[r], loads * 16)
                pe.wait_ge(block_added, f + 1)
                for t in range(TILES):
                    last = nc.tensor.matmul(dense_ps[r][0:D + 1, 0:WB], x1_nodes[:, t, :], blocks_in[:, r, t, :],
                                            start=(t == 0), stop=(t == TILES - 1))
                last.then_inc(block_summed, 1)

            def sum_all(layer, k):
                kk = k + passes if layer else k
                step0 = kk * STEPS
                use0 = [kk * PER_PASS[s] for s in range(U)]

                def back(i, s, chunks, count, beside=None):
                    sum_group(layer, step0 + i * U + s, s, use0[s] + i * WHOLE + 16 * chunks, chunks, count, 1, beside)

                if layer == 1:
                    with pe.Fori(0, ITERS) as i:
                        for s in range(U):
                            back(i, s, CH, 1)
                    back(ITERS, 0, TAIL, U)
                    return

                def turn(i, s, chunks, count):
                    turn_types(step0 + i * U + s, s, chunks, count)

                def look_up(i, s, chunks, count):
                    look_up_coefs(step0 + i * U + s, s, chunks, count)

                for s in range(U):
                    turn(0, s, CH, 1)
                    if s == 2:
                        back(0, 0, CH, 1)
                    look_up(0, s, CH, 1)
                with pe.Fori(1, ITERS) as i:
                    for s in range(U):
                        turn(i, s, CH, 1)
                        if s < 2:
                            back(i - 1, s + 1, CH, 1, (k, i - 1, DENSE_OF[s]))
                        else:
                            back(i, 0, CH, 1, (k, i - 1, DENSE_OF[s]))
                        look_up(i, s, CH, 1)
                turn(ITERS, 0, TAIL, U)
                back(ITERS - 1, 1, CH, 1, (k, ITERS - 1, range(0, CH)))
                look_up(ITERS, 0, TAIL, U)
                back(ITERS - 1, 2, CH, 1, (k, ITERS - 1, range(CH, DENSE)))
                back(ITERS, 0, TAIL, U)

            for layer in range(2):
                if layer == 0:
                    with pe.Fori(0, passes) as k:
                        sum_all(0, k)
                    pe.wait_ge(checked, passes)
                    pe.wait_ge(chunk_copied, passes * DENSE_CHUNKS + FREE_BANKS)
                    nc.tensor.matmul(node_ps[:, 0:1], ones[:, :], n_broken[:, :], start=True, stop=True).then_inc(broken_counted, 1)
                else:
                    slow, fast = load_loops(pe)
                    pe.wait_ge(part_a_normed, 1)
                    pe.wait_ge(part_b_normed, 1)
                    pe.wait_ge(self_added, -(-TILES // 4))
                    with pe.If(fast == 0), pe.Fori(0, slow) as k:
                        sum_all(1, k)
                    with pe.If(fast == 1):
                        step0 = passes * STEPS
                        use0 = [passes * PER_PASS[s] for s in range(U)]
                        with pe.Fori(0, FAST // SPAN6 - 1) as m:
                            for q in range(SPAN6):
                                f = m * SPAN6 + q
                                sum_block(f, q % 2, m * (SPAN6 // 2) + (q // 2 + 1))
                                sum_group(1, step0 + f * U, q % U, use0[q % U] + m * (SPAN6 // U * WHOLE) + (q // U + 1) * WHOLE, CH, U, U)
                        for f in range(FAST - SPAN6, ITERS):
                            sum_block(f, f % 2, f // 2 + 1)
                            sum_group(1, step0 + f * U, f % U, use0[f % U] + (f // U + 1) * WHOLE, CH, U, U)
                        sum_group(1, step0 + ITERS * U, ITERS % U, use0[ITERS % U] + ITERS // U * WHOLE + 16 * TAIL, TAIL, U, U)
                    pe.wait_ge(block_added, fast * ITERS + FREE_BANKS)
                pe.wait_ge(window_added, (passes * 2 if layer else passes) * STEPS + FREE)
                if layer:
                    for t in range(TILES):
                        last = nc.tensor.matmul(node_ps[:, t:t + 1], acc1[:, t * P:(t + 1) * P], deg_col[:, :], start=True, stop=True)
                    last.then_inc(degs_out, 1)
                for b in range(BATCHES):
                    bank = sums_ps[b % U]
                    if b >= U:
                        pe.wait_ge(nodes_read, BATCHES * layer + b - U + 1)
                    for t in range(BATCH):
                        cols = slice((b * BATCH + t) * P, (b * BATCH + t + 1) * P)
                        to = bank[:, t * D:(t + 1) * D]
                        if layer == 0:
                            for c in range(HALF):
                                last = nc.tensor.matmul(to, acc0[:, c, cols], w0_sb[:, c, :], start=(c == 0), stop=(c == HALF - 1))
                        else:
                            last = nc.tensor.matmul(to, acc1[0:D, cols], w1_sb[0:D, :], start=True, stop=True)
                    last.then_inc(nodes_out, 1)
                if layer == 0:
                    for t in range(TILES):
                        if t == 0:
                            pe.wait_ge(part_a_normed, 1)
                        if t == PARTS[1][0] * BATCH:
                            pe.wait_ge(part_b_normed, 1)
                        if t % 4 == 0 and t >= 4:
                            pe.wait_ge(self_added, t // 4)
                        last = nc.tensor.transpose(node_ps[0:D + 1, (t % 4) * P:(t % 4 + 1) * P], x1_nodes[:, t, :], ident[:, :])
                        if t % 4 == 3 or t == TILES - 1:
                            last.then_inc(x1_turned, 1)

        @block.vector
        def _(dve):
            nc.vector.memset(x_nodes[:, TILES - 1, :], 0.0)
            nc.vector.memset(wc_blocks[:, :], 0.0)
            nc.vector.memset(zero[:, :], 0.0)
            nc.vector.memset(deg_col[0:D, :], 0.0)
            nc.vector.memset(deg_col[D:D + 1, :], 1.0).then_inc(params_zeroed, 1)
            dve.sem_inc(window_added, FREE)
            dve.sem_inc(chunk_copied, FREE_BANKS)
            dve.sem_inc(block_added, FREE_BANKS)
            dve.sem_inc(coefs_weighted, 1)
            dve.sem_inc(factors_ready, 1)

            nc.vector.memset(lo[:, 1:2], 0.0).then_inc(start_step, 1)
            nc.vector.memset(hi[:, 1:2], 0.0).then_inc(start_step, 1)
            dve.wait_ge(start_step, 2)
            dve.wait_ge(dst_loaded, 48)
            for h in range(2):
                n = P if h == 0 else GROUPS - P
                nc.vector.tensor_reduce(lo[0:n, h:h + 1], dst_by_group[0:n, h, :], AX.X, ALU.min).then_inc(start_step, 1)
                nc.vector.tensor_reduce(hi[0:n, h:h + 1], dst_by_group[0:n, h, :], AX.X, ALU.max).then_inc(start_step, 1)
            dve.wait_ge(start_step, 6)
            nc.vector.tensor_tensor(span[:, :], hi[:, :], lo[:, :], ALU.subtract).then_inc(start_step, 1)
            dve.wait_ge(start_step, 7)
            dve.wait_ge(consts_ready, 6)
            for h in range(2):
                nc.vector.tensor_scalar(diag[:, h, :], ident[:, :], lo[:, h:h + 1], None, ALU.mult).then_inc(diag_ready, 1)
                nc.vector.tensor_scalar(diag[:, 2 + h, :], ident[:, :], span[:, h:h + 1], None, ALU.mult).then_inc(diag_ready, 1)
            nc.vector.tensor_copy(type_iota, type_iota_sb[:, :])
            nc.vector.tensor_copy(key_iota[:, :, :], key_iota_f)
            nc.vector.memset(hi_key[:, :, DENSE - 1:DENSE], -1.0)
            nc.vector.tensor_copy(win_iota, win_iota_sb[:, :]).then_inc(start_step, 1)
            dve.wait_ge(bases_spread, 1)
            nc.vector.tensor_reduce(max_span[:, :], node_ps[:, 256:256 + GROUPS], AX.X, ALU.max).then_inc(start_step, 1)
            dve.wait_ge(start_step, 9)
            nc.vector.tensor_scalar(further[:, :], win_steps[:, :], max_span[:, 0:1], None, ALU.is_le).then_inc(start_step, 1)
            dve.wait_ge(start_step, 10)
            nc.vector.tensor_reduce(n_further[:, :], further[:, :], AX.X, ALU.add).then_inc(start_step, 1)
            dve.wait_ge(start_step, 11)
            nc.vector.tensor_scalar(n_passes[0:1, :], n_further[0:1, :], 1.0, None, ALU.add).then_inc(passes_ready, 1)
            nc.vector.tensor_copy(first_base[:, :], node_ps[:, 0:GROUPS]).then_inc(start_step, 1)
            for a in (DST, TYPE):
                dve.wait_ge(rows_loaded[a], 32)
                rows = edge_rows[:, a, :, :]
                nc.vector.tensor_copy(rows[:, 0:BLOCKS - 1, :], rows[:, 0:BLOCKS - 1, :].bitcast(i32)).then_inc(rows_are_float[a], 1)
                nc.vector.tensor_copy(rows[0:LEFT, BLOCKS - 1, :], rows[0:LEFT, BLOCKS - 1, :].bitcast(i32)).then_inc(rows_are_float[a], 1)
            turned = TURNS
            for a in (DST, TYPE, WEIGHT):
                for t in range(0, BLOCKS, TURN):
                    n = min(TURN * P, CHUNKS - t * P)
                    dve.wait_ge(rows_turned, turned + 1)
                    nc.vector.tensor_copy(edges[:, a, t * P:t * P + n], turn_ps[turned % 2][:, 0:n]).then_inc(edges_ready, 1)
                    turned += 1
            dve.wait_ge(starts_spread, 1)
            for h, (i0, i1) in enumerate(START_BANKS):
                nc.vector.tensor_copy(starts[:, i0:i1, :], sums_ps[h][:, 0:(i1 - i0) * DENSE].rearrange("p (i j) -> p i j", j=DENSE)).then_inc(starts_ready, 1)
            dve.wait_ge(starts_ready, len(START_BANKS))
            nc.vector.tensor_tensor(hi_part[0:1, :, :], starts[0:1, :, :], starts[0:1, :, 0:1].to_broadcast([1, ITERS, DENSE]),
                                    ALU.subtract).then_inc(key_step, 1)
            dve.wait_ge(key_step, 1)
            nc.vector.tensor_scalar(spare[0:1, :, :], hi_part[0:1, :, :], 0.0, float(WB - SPREAD), ALU.max, ALU.min).then_inc(key_step, 1)
            dve.wait_ge(key_step, 2)
            nc.vector.tensor_copy(offsets[:, :, :], spare[0:1, :, :]).then_inc(starts_ready, 1)
            dve.wait_ge(params_loaded, 16 * N_PARAMS)
            nc.vector.tensor_scalar(neg_bias0[:, :], bias0_bc[:, :], -1.0, None, ALU.mult).then_inc(bias_ready, 1)
            dve.wait_ge(edges_ready, 3 * TURNS)
            dve.wait_ge(bias_ready, 1)
            dve.wait_ge(start_step, 12)
            dve.wait_ge(acc_zeroed, 1)
            dve.wait_ge(passes_ready, 1)
            passes = dve.value_load(n_passes[0:1, 0:1], min_val=1, max_val=EXTRA + 1)

            def make_keys(k, part, i0, i1):
                its = slice(i0, i1)
                of_chunks = edges[:, :, i0 * U * CH:i1 * U * CH].rearrange("p a (i c) -> p a i c", c=U * CH)
                sources, dests, weights = (of_chunks[:, a, :, 0:DENSE] for a in (SRC, DST, WEIGHT))
                hi, rest, at_node = hi_part[:, its, :], spare[:, its, :], place[:, its, :]
                to_next = at_node[:, :, 1:DENSE]
                w0_p, w1_p, w2_p = (w_part[w][:, its, :] for w in range(3))
                done = (k * 2 + part) * KEY_STEPS + 2
                at = [0]

                def step(instruction):
                    at[0] += 1
                    instruction.then_inc(key_step, 1)
                    dve.wait_ge(key_step, done + at[0])

                step(nc.vector.tensor_scalar(rest, sources, 1.0 / P, -(P - 1) / (2.0 * P), ALU.mult, ALU.add))
                step(nc.vector.tensor_scalar(rest, rest, ROUND, None, ALU.add))
                step(nc.vector.tensor_scalar(hi, rest, ROUND, None, ALU.subtract))
                step(nc.vector.scalar_tensor_tensor(lo_key[:, its, :], hi, -float(P), sources, ALU.mult, ALU.add))
                step(nc.vector.tensor_tensor(at_node, dests, starts[:, its, :], ALU.subtract))
                step(nc.vector.tensor_reduce(greatest[:, 0, part:part + 1], at_node, AX.XY, ALU.max))
                step(nc.vector.tensor_reduce(least[:, 0, part:part + 1], at_node, AX.XY, ALU.min))
                step(nc.vector.scalar_tensor_tensor(node_key[:, its, :], hi, float(SPREAD), at_node, ALU.mult, ALU.add))
                step(nc.vector.tensor_tensor(to_next, starts[:, its, 1:DENSE], dests[:, :, 0:DENSE - 1], ALU.subtract))
                step(nc.vector.tensor_reduce(greatest[:, 1, part:part + 1], to_next, AX.XY, ALU.max))
                step(nc.vector.tensor_reduce(least[:, 1, part:part + 1], to_next, AX.XY, ALU.min))
                step(nc.vector.scalar_tensor_tensor(hi_key[:, its, 0:DENSE - 1], to_next, -float(P), hi[:, :, 0:DENSE - 1], ALU.mult, ALU.add))
                step(nc.vector.tensor_tensor(to_next, starts[:, its, 1:DENSE], starts[:, its, 0:DENSE - 1], ALU.subtract))
                step(nc.vector.tensor_reduce(least[:, 2, part:part + 1], to_next, AX.XY, ALU.min))
                step(nc.vector.tensor_tensor(at_node[:, :, 0], starts[:, its, DENSE - 1], starts[:, its, 0], ALU.subtract))
                step(nc.vector.tensor_reduce(greatest[:, 2, part:part + 1], at_node[:, :, 0], AX.X, ALU.max))
                step(nc.vector.tensor_reduce(least[:, 3, part:part + 1], at_node[:, :, 0], AX.X, ALU.min))
                step(nc.vector.tensor_copy(w0_p, weights))
                step(nc.vector.tensor_tensor(rest, weights, w0_p, ALU.subtract))
                step(nc.vector.tensor_copy(w1_p, rest))
                step(nc.vector.tensor_tensor(w2_p, rest, w1_p, ALU.subtract))
                if part == 1:
                    for c, most in enumerate((SPREAD - 1, SPREAD, WB - SPREAD)):
                        nc.vector.tensor_scalar(broken[:, c, :], greatest[:, c, :], float(most), None, ALU.is_gt)
                    for c, fewest in enumerate((0, 0, 1, LEAST - SPREAD)):
                        last = nc.vector.tensor_scalar(broken[:, 3 + c, :], least[:, c, :], float(fewest), None, ALU.is_lt)
                    step(last)
                    nc.vector.tensor_reduce(n_broken[:, :], broken[:, :, :], AX.XY, ALU.add).then_inc(checked, 1)
                else:
                    dve.sem_inc(key_step, 1)

            def make_hots(k, b, js):
                j0, j1 = js[0], js[-1] + 1
                q0, q1 = j0 // 2, j1 // 2
                n = (k * ITERS + b) * DENSE

                def compared(values):
                    return key_iota[:, 0:values, :].unsqueeze(1).to_broadcast([P, q1 - q0, values, 2])

                def keys(array, values):
                    of_pairs = array[:, bass.ds(b, 1), j0:j1].rearrange("p i (q t) -> p (i q) t", t=2)
                    return of_pairs.unsqueeze(2).to_broadcast([P, q1 - q0, values, 2])

                dve.wait_ge(dense_summed, n + min(j1 + 1, DENSE))
                nc.vector.tensor_tensor(lo_hot[:, 2, q0:q1, :, :], compared(P), keys(lo_key, P), ALU.is_equal).then_inc(lo_hots_ready, 1)
                nc.vector.tensor_tensor(carry_hot[:, q0:q1, :, :], compared(TILES), keys(hi_key, TILES), ALU.is_equal)
                nc.vector.tensor_tensor(node_hot[:, q0:q1, :, :], compared(KEYS), keys(node_key, KEYS), ALU.is_equal)
                dve.wait_ge(lo_hots_ready, (k * ITERS + b) * U + (DENSE_OF.index(js) + 1))
                for w in range(3):
                    last = nc.vector.tensor_tensor(lo_hot[:, w, q0:q1, :, :], lo_hot[:, 2, q0:q1, :, :], keys(w_part[w], P), ALU.mult)
                last.then_inc(hots_ready, len(js))

            def compare_types(step, g, s, chunks, count):
                cols = bass.ds(g * CH, chunks)
                nc.vector.tensor_tensor(type_hot[:, s, 0:chunks, :],
                                        edges[:, TYPE, cols].unsqueeze(2).to_broadcast([P, chunks, R]),
                                        type_iota.unsqueeze(1).to_broadcast([P, chunks, R]),
                                        ALU.is_equal).then_inc(types_hot, count)

            def weigh(layer, step, g, s, chunks, count, unit=1):
                cols = bass.ds(g * CH, chunks)
                dve.wait_ge(factors_ready, step + 1)
                nc.vector.tensor_tensor(hits[:, 0:chunks, :], win_iota.unsqueeze(1).to_broadcast([P, chunks, WIN]),
                                        local_dst[:, cols].unsqueeze(2).to_broadcast([P, chunks, WIN]),
                                        ALU.is_equal).then_inc(hits_ready, count)
                dve.wait_ge(group_summed, slot_is_free(step, unit))
                if layer == 0:
                    dve.wait_ge(coefs_ready, step + 1)
                    nc.vector.tensor_tensor(coef_w[:, s, 0:chunks, :],
                                            coefs_ps[:, 0:chunks * B].rearrange("p (c b) -> p c b", b=B),
                                            edges[:, WEIGHT, cols].unsqueeze(2).to_broadcast([P, chunks, B]),
                                            ALU.mult).then_inc(coefs_weighted, count)
                    dve.wait_ge(coefs_weighted, step + 2)
                    dve.wait_ge(hits_ready, step + 1)
                    nc.vector.tensor_tensor(factors[:, s, 0:chunks, :, :],
                                            hits[:, 0:chunks, :].unsqueeze(2).to_broadcast([P, chunks, B, WIN]),
                                            coef_w[:, s, 0:chunks, :].unsqueeze(3).to_broadcast([P, chunks, B, WIN]),
                                            ALU.mult).then_inc(factors_ready, count)
                else:
                    dve.wait_ge(hits_ready, step + 1)
                    nc.vector.tensor_tensor(factors[:, s, 0:chunks, 0, :], hits[:, 0:chunks, :],
                                            edges[:, WEIGHT, cols].unsqueeze(2).to_broadcast([P, chunks, WIN]),
                                            ALU.mult).then_inc(factors_ready, count)

            def add_window(layer, step, g, s, count, blocks=None):
                node = dve.value_load(base_int[0:1, bass.ds(g, 1)], min_val=0, max_val=N)
                dve.wait_ge(group_summed, step + 1 + FREE)
                dve.wait_ge(window_added, step + FREE)
                if blocks is not None:
                    dve.wait_ge(block_added, blocks + FREE_BANKS)
                if layer == 0:
                    nc.vector.tensor_tensor(acc0[:, :, bass.ds(node, WIN)], acc0[:, :, bass.ds(node, WIN)],
                                            sums_ps[s][:, 0:HALF * WIN].rearrange("p (b w) -> p b w", b=HALF),
                                            ALU.add).then_inc(window_added, count)
                else:
                    nc.vector.tensor_tensor(acc1[:, bass.ds(node, WIN)], acc1[:, bass.ds(node, WIN)],
                                            sums_ps[s][0:D + 1, 0:WIN], ALU.add).then_inc(window_added, count)

            def first_windows():
                whole = (GROUPS - 1) * CH
                nc.vector.tensor_copy(base[:, :], first_base[0:1, :]).then_inc(base_ready, 1)
                nc.vector.tensor_copy(base_int[:, :], first_base[0:1, :]).then_inc(base_ready, 1)
                nc.vector.tensor_tensor(local_dst[:, 0:whole].rearrange("p (g c) -> p g c", c=CH),
                                        edges[:, DST, 0:whole].rearrange("p (g c) -> p g c", c=CH),
                                        first_base[:, 0:GROUPS - 1].unsqueeze(2).to_broadcast([P, GROUPS - 1, CH]),
                                        ALU.subtract).then_inc(base_ready, 1)
                nc.vector.tensor_tensor(local_dst[:, whole:CHUNKS], edges[:, DST, whole:CHUNKS],
                                        first_base[:, GROUPS - 1:GROUPS].to_broadcast([P, TAIL]),
                                        ALU.subtract).then_inc(base_ready, 1)

            def norm_part(layer, part):
                b0, b1 = PARTS[part]
                ts = slice(b0 * BATCH, b1 * BATCH)
                done = 10 * (2 * layer + part)
                dve.wait_ge(stats_ready, BATCHES * layer + b1)

                def step(instruction, n, wait=True):
                    instruction.then_inc(norm_step, 1)
                    if wait:
                        dve.wait_ge(norm_step, done + n)

                step(nc.vector.tensor_tensor(half_diff[:, ts], stats[:, ts, 1], stats[:, ts, 4], ALU.subtract), 1, False)
                step(nc.vector.tensor_tensor(var_eps[:, ts], stats[:, ts, 2], stats[:, ts, 5], ALU.add), 2, False)
                step(nc.vector.tensor_tensor(mean[:, ts], stats[:, ts, 1], stats[:, ts, 4], ALU.add), 3)
                step(nc.vector.scalar_tensor_tensor(half_diff[:, ts], half_diff[:, ts], 0.25, half_diff[:, ts], ALU.mult, ALU.mult), 4, False)
                step(nc.vector.tensor_scalar(var_eps[:, ts], var_eps[:, ts], 1.0 / D, EPS, ALU.mult, ALU.add), 5, False)
                step(nc.vector.tensor_scalar(mean[:, ts], mean[:, ts], 0.5, None, ALU.mult), 6)
                nc.vector.tensor_tensor(var_eps[:, ts], var_eps[:, ts], half_diff[:, ts], ALU.add).then_inc(var_ready, 1)
                dve.wait_ge(std_ready, 2 * layer + part + 1)
                step(nc.vector.reciprocal(rstd[:, ts], std[:, ts]), 7)
                step(nc.vector.tensor_tensor(newton[:, ts], rstd[:, ts], rstd[:, ts], ALU.mult), 8)
                step(nc.vector.scalar_tensor_tensor(newton[:, ts], newton[:, ts], -0.5, var_eps[:, ts], ALU.mult, ALU.mult), 9)
                step(nc.vector.scalar_tensor_tensor(rstd[:, ts], newton[:, ts], 1.5, rstd[:, ts], ALU.add, ALU.mult), 10)
                if part == 0:
                    nc.vector.scalar_tensor_tensor(neg_mean_rstd[:, ts], mean[:, ts], -1.0, rstd[:, ts],
                                                   ALU.mult, ALU.mult).then_inc(norm_ready, 1)
                else:
                    to = h_nodes if layer else x1_nodes
                    for t in range(b0 * BATCH, b1 * BATCH):
                        last = nc.vector.tensor_scalar(to[:, t, 0:D], h_nodes[:, t, :], mean[:, t:t + 1],
                                                       rstd[:, t:t + 1], ALU.subtract, ALU.mult)
                    last.then_inc(part_b_normed, 1)

            def weigh_all(layer, k):
                kk = k + passes if layer else k
                step0 = kk * STEPS
                dve.wait_ge(base_ready, kk * 3 + 4 + 4 * layer)

                def types(i, s, chunks, count):
                    compare_types(step0 + i * U + s, i * U + s, s, chunks, count)

                def front(i, s, chunks, count):
                    weigh(layer, step0 + i * U + s, i * U + s, s, chunks, count)

                def back(i, s, count):
                    add_window(layer, step0 + i * U + s, i * U + s, s, count)

                def hots(b, s):
                    make_hots(k, b, DENSE_OF[s])

                def iteration(i, keys=False):
                    for s in range(U):
                        types(i, s, CH, 1)
                        if s == 0:
                            front(i - 1, U - 1, CH, 1)
                        else:
                            front(i, s - 1, CH, 1)
                        back(i - 1, s, 1)
                        if s == U - 1 and keys:
                            dve.wait_ge(dense_summed, k * DENSE_CHUNKS + DENSE + FREE_HOTS)
                            make_keys(k, 1, 1, ITERS)
                        hots(i - 1 if s < U - 1 else i, (s + 1) % U)

                if layer == 1:
                    for s in range(U):
                        front(0, s, CH, 1)
                        back(0, s, 1)
                    with dve.Fori(1, ITERS) as i:
                        for s in range(U):
                            front(i, s, CH, 1)
                            back(i, s, 1)
                    front(ITERS, 0, TAIL, U)
                    back(ITERS, 0, U)
                else:
                    for s in range(U):
                        types(0, s, CH, 1)
                        if s > 0:
                            front(0, s - 1, CH, 1)
                    dve.wait_ge(dense_summed, k * DENSE_CHUNKS + FREE_HOTS)
                    dve.wait_ge(starts_ready, 4)
                    make_keys(k, 0, 0, 1)
                    hots(0, 0)
                    iteration(1, keys=True)
                    with dve.Fori(2, ITERS) as i:
                        iteration(i)
                    types(ITERS, 0, TAIL, U)
                    front(ITERS - 1, 2, CH, 1)
                    back(ITERS - 1, 0, 1)
                    hots(ITERS - 1, 1)
                    hots(ITERS - 1, 2)
                    front(ITERS, 0, TAIL, U)
                    back(ITERS - 1, 1, 1)
                    back(ITERS - 1, 2, 1)
                    back(ITERS, 0, U)
                dve.wait_ge(window_added, step0 + STEPS + FREE)
                nc.vector.tensor_scalar(base[:, :], base[:, :], float(WIN), float(N), ALU.add, ALU.min).then_inc(base_ready, 1)
                nc.vector.tensor_scalar(local_dst[:, :], local_dst[:, :], float(WIN), None, ALU.subtract).then_inc(base_ready, 1)
                dve.wait_ge(base_ready, kk * 3 + 6 + 4 * layer)
                nc.vector.tensor_copy(base_int[:, :], base[:, :]).then_inc(base_ready, 1)

            def add_block(f, r, step):
                node = dve.value_load(base_int[0:1, bass.ds(f * U, 1)], min_val=0, max_val=N)
                dve.wait_ge(block_summed, f + 1 + FREE_BANKS)
                dve.wait_ge(window_added, step + FREE)
                nc.vector.tensor_tensor(acc1[:, bass.ds(node, WB)], acc1[:, bass.ds(node, WB)],
                                        dense_ps[r][0:D + 1, 0:WB], ALU.add).then_inc(block_added, 1)

            first_windows()
            for layer in range(2):
                if layer == 0:
                    with dve.Fori(0, passes) as k:
                        weigh_all(0, k)
                else:
                    slow, fast = load_loops(dve)
                    with dve.If(fast == 0), dve.Fori(0, slow) as k:
                        weigh_all(1, k)
                    with dve.If(fast == 1):
                        step0 = passes * STEPS
                        def with_block(f, s, r):
                            weigh(1, step0 + f * U, f * U + (U - 1), s, CH, U, U)
                            add_block(f, r, step0 + f * U)
                            add_window(1, step0 + f * U, f * U + (U - 1), s, U, f + 1)

                        with dve.Fori(0, FAST // SPAN6 - 1) as m:
                            for q in range(SPAN6):
                                with_block(m * SPAN6 + q, q % U, q % 2)
                        for f in range(FAST - SPAN6, ITERS):
                            with_block(f, f % U, f % 2)
                        weigh(1, step0 + ITERS * U, ITERS * U, ITERS % U, TAIL, U, U)
                        add_window(1, step0 + ITERS * U, ITERS * U, ITERS % U, U, ITERS)

                dve.wait_ge(bias_added, layer + 1)
                if layer:
                    dve.wait_ge(degs_out, 1)
                    nc.vector.tensor_scalar(has_deg[:, :], node_ps[:, 0:TILES], 0.0, None, ALU.is_gt).then_inc(deg_step, 1)
                    nc.vector.tensor_scalar(inv_deg[:, :], node_ps[:, 0:TILES], TINY, None, ALU.max).then_inc(deg_step, 1)
                    dve.wait_ge(deg_step, 2)
                    nc.vector.reciprocal(inv_deg[:, :], inv_deg[:, :]).then_inc(deg_step, 1)
                    dve.wait_ge(deg_step, 3)
                    nc.vector.tensor_tensor(inv_deg[:, :], inv_deg[:, :], has_deg[:, :], ALU.mult).then_inc(deg_step, 1)
                    dve.wait_ge(deg_step, 4)
                else:
                    dve.wait_ge(base_ready, passes * 3 + 4)
                    first_windows()
                    dve.wait_ge(broken_counted, 1)
                    nc.vector.tensor_tensor(not_fast[:, :], node_ps[0:1, 0:1], n_further[0:1, :], ALU.add).then_inc(loop_step, 1)
                    dve.wait_ge(loop_step, 1)
                    nc.vector.tensor_scalar(not_fast[:, :], not_fast[:, :], 0.0, None, ALU.is_gt).then_inc(loop_step, 1)
                    dve.wait_ge(loop_step, 2)
                    nc.vector.scalar_tensor_tensor(loops[:, 0:1], n_further[0:1, :], 1.0, not_fast[:, :], ALU.add, ALU.mult)
                    nc.vector.tensor_scalar(loops[:, 1:2], not_fast[:, :], -1.0, 1.0, ALU.mult, ALU.add).then_inc(loops_ready, 1)
                    for r in range(2):
                        dve.wait_ge(blocks_stored[r], passes * BLOCKS_OF[r] * 16 + 16)
                    dve.wait_ge(base_ready, passes * 3 + 8)
                    nc.vector.memset(x1_nodes[:, :, D:D + 1], 1.0)
                for b in range(BATCHES):
                    batch = BATCHES * layer + b
                    tiles = slice(b * BATCH, (b + 1) * BATCH)
                    rows = sums_ps[b % U][:, 0:BATCH * D].rearrange("p (t f) -> p t f", t=BATCH)
                    dve.wait_ge(nodes_out, batch + 1)
                    if layer == 0:
                        nc.vector.tensor_tensor(h_nodes[:, tiles, :], rows, neg_bias0[:, :].unsqueeze(1).to_broadcast([P, BATCH, D]),
                                                ALU.max).then_inc(nodes_read, 1)
                        dve.wait_ge(nodes_read, batch + 1)
                        nc.vector.tensor_tensor(h_nodes[:, tiles, :], h_nodes[:, tiles, :], x_nodes[:, tiles, :], ALU.add).then_inc(nodes_added, 1)
                    else:
                        for t in range(BATCH):
                            last = nc.vector.scalar_tensor_tensor(h_nodes[:, b * BATCH + t, :], rows[:, t, :],
                                                                  inv_deg[:, b * BATCH + t:b * BATCH + t + 1],
                                                                  x_nodes[:, b * BATCH + t, :], ALU.mult, ALU.add)
                            if t == BATCH - 1:
                                last.then_inc(nodes_read, 1)
                    dve.wait_ge(nodes_read, batch + 1)
                    dve.wait_ge(nodes_added, min(batch + 1, BATCHES))
                    for t in range(b * BATCH, (b + 1) * BATCH):
                        last = nc.vector.bn_stats(stats[:, t, :], h_nodes[:, t, :])
                    last.then_inc(stats_ready, 1)
                    if b + 1 == PARTS[0][1]:
                        norm_part(layer, 0)
                norm_part(layer, 1)
                if layer == 0:
                    for q in range(-(-TILES // 4)):
                        n = min(4, TILES - 4 * q) * P
                        dve.wait_ge(x1_turned, q + 1)
                        nc.vector.tensor_copy(acc1[:, q * 4 * P:q * 4 * P + n], node_ps[0:D + 1, 0:n]).then_inc(self_added, 1)
                    dve.wait_ge(self_added, -(-TILES // 4))
                    dve.wait_ge(part_a_normed, 1)
                    dve.wait_ge(part_b_normed, 1)


_INS = ['x', 'src', 'dst', 'edge_type_32', 'edge_weight', 'L0_gnn_weight', 'L0_gnn_w_comp', 'L0_gnn_bias', 'L1_gnn_W', 'L1_gnn_b']
_FILL = {'src': 0, 'dst': N - 1, 'edge_type_32': 0, 'edge_weight': 0}


def kernel(**inputs):
    import numpy as _np
    import concourse.bacc as _bacc
    from concourse import mybir as _mybir
    from concourse.bass_utils import run_bass_kernel_spmd as _run

    nc = _bacc.Bacc("TRN2", target_bir_lowering=False, num_devices=1)
    arrays, args = {}, []
    for name in _INS:
        a = _np.ascontiguousarray(inputs[name])
        if name in _FILL:
            a = _np.concatenate([a, _np.full((CHUNKS * P - E,), _FILL[name], a.dtype)])
        arrays[f"in_{name}"] = a
        args.append(nc.dram_tensor(f"in_{name}", a.shape, _mybir.dt.from_np(a.dtype), kind="ExternalInput").ap())
    y = nc.dram_tensor("out_y", (N, D), _mybir.dt.float32, kind="ExternalOutput").ap()
    gnn_two_layers(nc, *args, y)
    r = _run(nc, [arrays], core_ids=[0])
    return r.results[0]["out_y"]
```

```python
import concourse.bass as bass
from concourse import mybir
from contextlib import ExitStack


N = 6250
E = 200000
D = 64
R = 32
B = 4
P = 128
CH = 8
U = 3
WIN = 44
CHUNKS = -(-E // P)
ITERS = CHUNKS // (CH * U)
TAIL = CHUNKS - ITERS * CH * U
GROUPS = ITERS * U + 1
BLOCKS = -(-CHUNKS // P)
LEFT = CHUNKS - (BLOCKS - 1) * P
TURN = 4
TURNS = -(-BLOCKS // TURN)
STEPS = (ITERS + 1) * U
TILES = -(-N // P)
NPAD = TILES * P + max(WIN, 72)
BATCH = 7
BATCHES = TILES // BATCH
HALF = B // 2
POOL_NORMS = (14, 6 * BATCH)
PARTS = [[(0, 6, 0), (6, BATCHES, 0)],
         [(0, 2, BATCH), (2, 4, 0), (4, 6, 0), (6, BATCHES, 0)]]
FIRST_EARLY = ITERS - (BATCHES - 1) // 2
EXTRA = -(-N // WIN)
DENSE = 16
DENSE_CHUNKS = ITERS * DENSE
SPREAD = 7
WB = 72
LEAST = 60
BLK = TILES * WB
KEYS = TILES * SPREAD
DENSE_OF = [range(0, 6), range(6, 10), range(10, 16)]
PAIRS = DENSE // 2
BLOCKS_OF = [(ITERS + 1) // 2, ITERS // 2]
FIRST_KEYS = 5
KEY_PIECE = 6
ROUND = 12582912.0
FAST = ITERS + 1
SPAN6 = 6
PEEL = 3 * SPAN6
EARLY = {FAST - 2 * BATCHES + 2 * b: b for b in range(BATCHES - 1)}
EPS = 1e-5
TINY = 1.1754943508222875e-38
assert 0 < TAIL <= CH and TILES == BATCH * BATCHES and GROUPS <= 2 * P
assert (BATCHES - 1) % 2 == 0
assert (ITERS - FIRST_KEYS) % KEY_PIECE == 0
assert CH * U > DENSE and (ITERS - 1) % 2 == 0 and FAST % SPAN6 == 0 and WB <= NPAD - TILES * P <= 2 * BLK
LAST = N - (TILES - 1) * P


def gnn_two_layers(nc, x, src, dst, etype, eweight, w0, w_comp, bias0, w1, bias1, out):
    f32 = mybir.dt.float32
    i32 = mybir.dt.int32
    bf16 = mybir.dt.bfloat16
    f16 = mybir.dt.float16
    ALU = mybir.AluOpType
    ACT = mybir.ActivationFunctionType
    AX = mybir.AxisListType

    table = nc.dram_tensor("x1_table", (TILES * P, D), f32, kind="Internal").ap()
    block_table = nc.dram_tensor("block_table", (ITERS * P, BLK), f32, kind="Internal").ap()
    edge_arrays = (src, dst, etype, eweight)
    SRC, DST, TYPE, WEIGHT = range(4)

    ctx = ExitStack()
    with ctx:
        def sb(name, shape, dt=f32):
            return ctx.enter_context(nc.sbuf_tensor(name, shape, dt))

        def pb(name, shape):
            return ctx.enter_context(nc.psum_tensor(name, shape, f32))

        def sem(name):
            return ctx.enter_context(nc.semaphore(name))

        ident = sb("ident", [P, P])
        ones = sb("ones", [P, P])
        type_iota_sb = sb("type_iota_sb", [P, R])
        win_iota_sb = sb("win_iota_sb", [P, WIN])
        lo = sb("lo", [P, 2])
        hi = sb("hi", [P, 2])
        span = sb("span", [P, 2])
        first_base = sb("first_base", [P, GROUPS])
        base = sb("base", [1, GROUPS])
        base_int = sb("base_int", [1, GROUPS], i32)
        max_span = sb("max_span", [P, 1])
        n_further = sb("n_further", [P, 1])
        n_passes = sb("n_passes", [1, 1], i32)
        edges = sb("edges", [P, 4, CHUNKS])
        local_dst = sb("local_dst", [P, CHUNKS])
        idx = sb("idx", [P, U, CH], i32)
        gathered_rows = sb("gathered_rows", [P, U, CH, D + 4])
        type_hot = sb("type_hot", [P, U, CH, R])
        type_hot_t = sb("type_hot_t", [P, 2, P])
        coef_w = sb("coef_w", [P, U, CH, B])
        factors_room = sb("factors_room", [P, U * CH * B * WIN])
        factors = factors_room[:, :].rearrange("p (s c b w) -> p s c b w", s=U, c=CH, b=B)
        dst_by_group = factors_room[:, 0:2 * P * CH].bitcast(i32).rearrange("p (h e) -> p h e", h=2)
        starts = sb("starts", [P, ITERS, DENSE])
        offsets = sb("offsets", [1, ITERS, DENSE], i32)
        hi_key = sb("hi_key", [P, ITERS, DENSE], f16)
        lo_key = sb("lo_key", [P, ITERS, DENSE], f16)
        node_key = sb("node_key", [P, ITERS, DENSE], f16)
        w_part = [sb(f"w_part{w}", [P, ITERS, DENSE], bf16) for w in range(3)]
        key_iota = sb("key_iota", [P, KEYS, 2], f16)
        key_iota_f = factors_room[:, 2 * P * CH:2 * P * CH + 2 * KEYS].rearrange("p (v t) -> p v t", t=2)
        diag = factors_room[:, 3 * P * CH:3 * P * CH + 4 * P].rearrange("p (d e) -> p d e", d=4)
        win_steps = factors_room[:, 3 * P * CH + 4 * P:3 * P * CH + 4 * P + EXTRA]
        further = factors_room[:, 3 * P * CH + 4 * P + EXTRA:3 * P * CH + 4 * P + 2 * EXTRA]
        lo_room = sb("lo_room", [P, 3 * PAIRS * P])
        node_room = sb("node_room", [P, PAIRS * KEYS])
        lo_hot = lo_room[:, :].bitcast(bf16).rearrange("p (w q e t) -> p w q e t", w=3, q=PAIRS, t=2)
        node_hot = node_room[:, :].bitcast(bf16).rearrange("p (q v t) -> p q v t", q=PAIRS, t=2)
        carry_hot = sb("carry_hot", [P, PAIRS, TILES, 2], bf16)
        start_room = lo_room[0:1, 0:DENSE_CHUNKS].rearrange("p (i j) -> p i j", j=DENSE)
        key_room = [sb(f"key_room{q}", [P, KEY_PIECE, DENSE]) for q in range(3)]
        found = sb("found", [P, 7])
        greatest = sb("greatest", [P, 3])
        least = sb("least", [P, 4])
        broken = sb("broken", [P, 7 + len(EARLY)])
        least_behind = sb("least_behind", [1, BATCHES - 1])
        reached = sb("reached", [1, BATCHES - 1])
        not_early = sb("not_early", [1, 1])
        early_flag = sb("early_flag", [1, 1], i32)
        least_left = sb("least_left", [P, len(EARLY)])
        n_broken = sb("n_broken", [P, 1])
        not_fast = sb("not_fast", [1, 1])
        loops = sb("loops", [1, 2], i32)
        zero = sb("zero", [P, 1])
        wc_blocks = sb("wc_blocks", [P, 4 * B])
        w0_sb = sb("w0_sb", [P, HALF, D])
        w1_deg = sb("w1_deg", [D + 1, D + 1])
        bias0_bc = sb("bias0_bc", [P, D])
        neg_bias0 = sb("neg_bias0", [P, D])
        bias1_bc = sb("bias1_bc", [P, D])
        x_nodes = sb("x_nodes", [P, TILES, D])
        room = sb("room", [P, 2 * BLK])
        edge_rows = room[:, 0:4 * BLOCKS * P].rearrange("p (a t e) -> p a t e", a=4, t=BLOCKS)
        blocks_out = room[:, :].rearrange("p (b h w) -> p b h w", b=2, h=TILES)
        x1_nodes = room[:, 0:TILES * (D + 1)].rearrange("p (t f) -> p t f", f=D + 1)
        h_nodes = room[:, BLK:BLK + TILES * D].rearrange("p (t f) -> p t f", f=D)
        acc_room = sb("acc_room", [P, NPAD + 2 * BLK])
        acc0 = acc_room[:, 0:HALF * NPAD].rearrange("p (b n) -> p b n", b=HALF)
        acc1 = acc_room[0:D + 1, 0:NPAD]
        x1_new = acc0[:, 1, 0:TILES * P].rearrange("p (t q) -> p t q", q=P)[:, :, 0:D]
        blocks_in = acc_room[:, NPAD:NPAD + 2 * BLK].rearrange("p (b h w) -> p b h w", b=2, h=TILES)
        stats = sb("stats", [P, TILES, 6])
        mean = sb("mean", [P, TILES])
        half_diff = sb("half_diff", [P, TILES])
        var_eps = sb("var_eps", [P, TILES])
        std = sb("std", [P, TILES])
        rstd = sb("rstd", [P, TILES])
        newton = sb("newton", [P, TILES])
        neg_mean_rstd = sb("neg_mean_rstd", [P, TILES])
        has_deg = sb("has_deg", [P, TILES])
        inv_deg = sb("inv_deg", [P, TILES])

        types_ps = pb("types_ps", [P, 512])
        coefs_ps = pb("coefs_ps", [P, 512])
        turn_ps = [types_ps, coefs_ps]
        dve_ps = pb("dve_ps", [P, 512])
        type_iota = dve_ps[:, 0:R]
        win_iota = dve_ps[:, R:R + WIN]
        hits = dve_ps[:, 128:128 + CH * WIN].rearrange("p (c w) -> p c w", c=CH)
        sums_ps = [pb(f"sums_ps{s}", [P, 512]) for s in range(U)]
        node_ps = pb("node_ps", [P, 512])
        early_ps = [types_ps, coefs_ps]
        self_ps = [node_ps, *sums_ps]
        dense_ps = [pb("dense_ps", [P, 512]), node_ps]

        x_loaded = sem("x_loaded")
        params_loaded = sem("params_loaded")
        dst_loaded = sem("dst_loaded")
        consts_ready = sem("consts_ready")
        pool_step = sem("pool_step")
        params_zeroed = sem("params_zeroed")
        diag_ready = sem("diag_ready")
        bases_spread = sem("bases_spread")
        passes_ready = sem("passes_ready")
        start_step = sem("start_step")
        base_ready = sem("base_ready")
        rows_loaded = [sem(f"rows_loaded{a}") for a in range(4)]
        rows_are_float = [sem(f"rows_are_float{a}") for a in range(3)]
        sources_ready = sem("sources_ready")
        acc_zeroed = sem("acc_zeroed")
        rows_turned = sem("rows_turned")
        edges_ready = sem("edges_ready")
        idx_ready = sem("idx_ready")
        gathers_begun = sem("gathers_begun")
        counts_reset = sem("counts_reset")
        passes_begun = sem("passes_begun")
        rows_gathered = [sem(f"rows_gathered{s}") for s in range(U)]
        types_hot = sem("types_hot")
        types_turned = sem("types_turned")
        types_copied = sem("types_copied")
        coefs_ready = sem("coefs_ready")
        dst_local = sem("dst_local")
        hits_ready = sem("hits_ready")
        coefs_weighted = sem("coefs_weighted")
        factors_ready = sem("factors_ready")
        group_summed = sem("group_summed")
        window_added = sem("window_added")
        nodes_out = sem("nodes_out")
        nodes_read = sem("nodes_read")
        nodes_added = sem("nodes_added")
        deg_step = sem("deg_step")
        stats_ready = sem("stats_ready")
        norm_step = sem("norm_step")
        var_ready = sem("var_ready")
        std_ready = sem("std_ready")
        norm_ready = sem("norm_ready")
        rstd_ready = sem("rstd_ready")
        bias_ready = sem("bias_ready")
        bias_added = sem("bias_added")
        x1_normed = [sem(f"x1_normed{p}") for p in range(len(PARTS[0]))]
        y_normed = [sem(f"y_normed{p}") for p in range(len(PARTS[1]))]
        part_normed = [x1_normed, y_normed]
        x1_step = sem("x1_step")
        x1_copied = sem("x1_copied")
        early_step = sem("early_step")
        early_ready = sem("early_ready")
        x1_turned = sem("x1_turned")
        self_added = sem("self_added")
        x1_stored = sem("x1_stored")
        starts_spread = sem("starts_spread")
        starts_copied = sem("starts_copied")
        starts_ready = sem("starts_ready")
        offsets_ready = sem("offsets_ready")
        room_zeroed = sem("room_zeroed")
        key_step = sem("key_step")
        keys_checked = sem("keys_checked")
        lo_hots_ready = sem("lo_hots_ready")
        hots_ready = sem("hots_ready")
        dense_summed = sem("dense_summed")
        chunk_copied = sem("chunk_copied")
        tail_zeroed = sem("tail_zeroed")
        blocks_stored = [sem(f"blocks_stored{r}") for r in range(2)]
        checked = sem("checked")
        least_left_found = sem("least_left_found")
        broken_counted = sem("broken_counted")
        loop_step = sem("loop_step")
        loops_ready = sem("loops_ready")
        block_loaded = [sem(f"block_loaded{r}") for r in range(2)]
        block_summed = sem("block_summed")
        block_added = sem("block_added")
        y_stored = sem("y_stored")

        block = ctx.enter_context(nc.Block())

        N_PARAMS = 4 + 2 + 1 + 2
        WHOLE = 16 * CH
        PER_PASS = [ITERS * WHOLE + (16 * TAIL if s == 0 else 0) for s in range(U)]
        FREE = 2 * U + 1
        FREE_BANKS = 2
        FREE_HOTS = DENSE

        def slot_is_free(step, count):
            return step + FREE - (U - 1) * count

        def load_loops(engine):
            engine.wait_ge(loops_ready, 1)
            return (engine.value_load(loops[0:1, 0:1], min_val=0, max_val=EXTRA + 1),
                    engine.value_load(loops[0:1, 1:2], min_val=0, max_val=1))

        def norm_shares(layer, part):
            b0, b1, on_act = PARTS[layer][part]
            return (on_act > 0) + 1 + ((layer, part) == (0, 0))

        def norm_steps(layer, part):
            return 11 + (PARTS[layer][part][2] > 0)

        def load_early(engine):
            engine.wait_ge(early_ready, 1)
            return engine.value_load(early_flag[0:1, 0:1], min_val=0, max_val=1)

        KEY_STEPS = 12
        KEY_PIECES = 2 + (ITERS - FIRST_KEYS) // KEY_PIECE
        START_ITERS = [(i0, min(i0 + 512 // DENSE, ITERS)) for i0 in range(0, ITERS, 512 // DENSE)]
        START_BANKS = [dense_ps[0], dense_ps[1], sums_ps[U - 1]]

        def load_rows(queue, a):
            to = edge_rows[:, a, :, :] if a == WEIGHT else edge_rows[:, a, :, :].bitcast(i32)
            rows = edge_arrays[a].rearrange("(c e) -> c e", e=P)
            whole = (BLOCKS - 1) * P
            queue.dma_start(to[:, 0:BLOCKS - 1, :], rows[0:whole, :].rearrange("(t p) e -> p t e", p=P)).then_inc(rows_loaded[a], 16)
            queue.wait_ge(room_zeroed, 1)
            queue.dma_start(to[0:LEFT, BLOCKS - 1, :], rows[whole:CHUNKS, :]).then_inc(rows_loaded[a], 16)

        @block.sync
        def _(sp):
            sp.dma_start(dst_by_group[:, 0, :], dst[0:P * P * CH].rearrange("(g e) -> g e", g=P)).then_inc(dst_loaded, 16)
            rest = GROUPS - 1 - P
            sp.dma_start(dst_by_group[0:rest, 1, :],
                         dst[P * P * CH:(GROUPS - 1) * P * CH].rearrange("(g e) -> g e", g=rest)).then_inc(dst_loaded, 16)
            sp.dma_start(dst_by_group[rest:rest + 1, 1, :],
                         dst[(CHUNKS - CH) * P:CHUNKS * P].rearrange("(g e) -> g e", g=1)).then_inc(dst_loaded, 16)
            for a in (DST, TYPE, WEIGHT):
                load_rows(sp, a)
            sp.wait_ge(params_zeroed, 1)
            for j in range(4):
                sp.dma_start(wc_blocks[R * j:R * j + R, B * j:B * j + B], w_comp[:, :]).then_inc(params_loaded, 16)
            for h in range(2):
                sp.dma_start(w0_sb[D * h:D * h + D, :, :], w0[HALF * h:HALF * h + HALF].rearrange("b i o -> i b o")).then_inc(params_loaded, 16)
            sp.dma_start(w1_deg[0:D, 0:D], w1[:, :]).then_inc(params_loaded, 16)
            sp.dma_start(bias0_bc[:, :], bias0.rearrange("(a o) -> a o", a=1).to_broadcast([P, D])).then_inc(params_loaded, 16)
            sp.dma_start(bias1_bc[:, :], bias1.rearrange("(a o) -> a o", a=1).to_broadcast([P, D])).then_inc(params_loaded, 16)
            sp.dma_start(x_nodes[:, 0:TILES - 1, :], x[0:(TILES - 1) * P, :].rearrange("(t p) f -> p t f", p=P)).then_inc(x_loaded, 16)
            sp.dma_start(x_nodes[0:LAST, TILES - 1, :], x[(TILES - 1) * P:N, :]).then_inc(x_loaded, 16)
            for r in range(2):
                sp.sem_inc(blocks_stored[r], 16)
            sp.wait_ge(passes_ready, 1)
            passes = sp.value_load(n_passes[0:1, 0:1], min_val=1, max_val=EXTRA + 1)

            def store_block(k, b, r):
                sp.wait_ge(chunk_copied, (k * ITERS + b) * DENSE + DENSE + FREE_BANKS)
                sp.dma_start(block_table[bass.ds(b * P, P), :], blocks_out[:, r, :, :].rearrange("p h w -> p (h w)")).then_inc(blocks_stored[r], 16)

            with sp.Fori(0, passes) as k:
                with sp.Fori(0, ITERS // 2) as m:
                    for r in range(2):
                        store_block(k, m * 2 + r, r)
                store_block(k, ITERS - 1, 0)
            for part, (b0, b1, _) in enumerate(PARTS[0]):
                sp.wait_ge(x1_normed[part], norm_shares(0, part))
                sp.dma_start(table[b0 * BATCH * P:b1 * BATCH * P, :].rearrange("(t p) f -> p t f", p=P),
                             x1_new[:, b0 * BATCH:b1 * BATCH, :]).then_inc(x1_stored, 16)
            slow, fast = load_loops(sp)
            sp.wait_ge(nodes_out, BATCHES)
            sp.wait_ge(x1_copied, 1)
            sp.wait_ge(x1_stored, 16 * len(PARTS[0]))

            def load_block(f, r):
                sp.wait_ge(block_summed, f + 1)
                sp.dma_start(blocks_in[:, r, :, :].rearrange("p h w -> p (h w)"), block_table[bass.ds(f * P, P), :]).then_inc(block_loaded[r], 16)

            with sp.If(fast == 1):
                with sp.Fori(0, (FAST - PEEL) // SPAN6) as m:
                    for q in range(SPAN6):
                        load_block(m * SPAN6 + q, q % 2)
                for f in range(FAST - PEEL, ITERS):
                    load_block(f, f % 2)
            for part, (b0, b1, _) in enumerate(PARTS[1]):
                sp.wait_ge(y_normed[part], norm_shares(1, part))
                t0, t1 = b0 * BATCH, min(b1 * BATCH, TILES - 1)
                sp.dma_start(out[t0 * P:t1 * P, :].rearrange("(t p) f -> p t f", p=P),
                             h_nodes[:, t0:t1, :]).then_inc(y_stored, 16)
            sp.dma_start(out[(TILES - 1) * P:N, :], h_nodes[0:LAST, TILES - 1, :]).then_inc(y_stored, 16)
            sp.wait_ge(y_stored, 16 * (len(PARTS[1]) + 1))

        @block.gpsimd
        def _(pool):
            nc.gpsimd.memset(ones[:, :], 1.0).then_inc(pool_step, 1)
            nc.gpsimd.memset(ident[:, :], 0.0).then_inc(pool_step, 1)
            pool.wait_ge(pool_step, 2)
            nc.gpsimd.affine_select(out=ident[:, :], in_=ident[:, :], compare_op=ALU.not_equal, fill=1.0, base=0,
                                    pattern=[[-1, P]], channel_multiplier=1).then_inc(consts_ready, 1)
            nc.gpsimd.iota(type_iota_sb[:, :], pattern=[[1, R]], base=0, channel_multiplier=0,
                           allow_small_or_imprecise_dtypes=True).then_inc(consts_ready, 1)
            nc.gpsimd.iota(win_iota_sb[:, :], pattern=[[1, WIN]], base=0, channel_multiplier=0,
                           allow_small_or_imprecise_dtypes=True).then_inc(consts_ready, 1)
            nc.gpsimd.iota(win_steps, pattern=[[WIN, EXTRA]], base=WIN, channel_multiplier=0,
                           allow_small_or_imprecise_dtypes=True).then_inc(consts_ready, 1)
            nc.gpsimd.memset(gathered_rows[:, :, :, D:D + 1], 1.0).then_inc(consts_ready, 1)
            nc.gpsimd.iota(key_iota_f, pattern=[[1, KEYS], [0, 2]], base=0, channel_multiplier=0,
                           allow_small_or_imprecise_dtypes=True).then_inc(consts_ready, 1)
            nc.gpsimd.memset(acc0[:, :, :], 0.0).then_inc(acc_zeroed, 1)
            pool.wait_ge(passes_ready, 1)
            passes = pool.value_load(n_passes[0:1, 0:1], min_val=1, max_val=EXTRA + 1)

            def gather_group(step, s, chunks, rows):
                pool.wait_ge(idx_ready, step + 1)
                pool.sem_inc(gathers_begun, 1)
                for j in range(chunks):
                    pool.indirect_dma_start(gathered_rows[:, s, j, 0:D], None, rows,
                                            bass.IndirectOffsetOnAxis(ap=idx[:, s, j:j + 1], axis=0)
                                            ).then_inc(rows_gathered[s], 16)

            pool.sem_inc(counts_reset, 1)

            def reset_counts(kk):
                pool.wait_ge(group_summed, kk * STEPS + FREE)
                pool.sem_inc(gathers_begun, 1)
                pool.inc_swdge_sem(rows_gathered, PER_PASS, mode="sub")
                pool.drain().then_inc(counts_reset, 1)

            def gather_all(layer, k):
                step0 = (k + passes if layer else k) * STEPS
                if layer:
                    reset_counts(k + passes)
                else:
                    with pool.If(k > 0):
                        reset_counts(k)
                rows = table[:, :] if layer else x[:, :]
                with pool.Fori(0, ITERS) as i:
                    for s in range(U):
                        gather_group(step0 + i * U + s, s, CH, rows)
                gather_group(step0 + ITERS * U, 0, TAIL, rows)

            with pool.Fori(0, passes) as k:
                gather_all(0, k)
            pool.wait_ge(rstd_ready, 1)
            ts, n = slice(*POOL_NORMS), POOL_NORMS[1] - POOL_NORMS[0]
            nc.gpsimd.tensor_tensor(x1_new[:, ts, :], x1_new[:, ts, :], mean[:, ts].unsqueeze(2).to_broadcast([P, n, D]),
                                    ALU.subtract).then_inc(pool_step, 1)
            pool.wait_ge(pool_step, 3)
            nc.gpsimd.tensor_tensor(x1_new[:, ts, :], x1_new[:, ts, :], rstd[:, ts].unsqueeze(2).to_broadcast([P, n, D]),
                                    ALU.mult).then_inc(x1_normed[0], 1)
            slow, fast = load_loops(pool)
            pool.wait_ge(x1_stored, 16 * len(PARTS[0]))
            with pool.If(fast == 0):
                with pool.Fori(0, slow) as k:
                    gather_all(1, k)
                pool.wait_ge(bias_added, 1)
                for b in range(BATCHES):
                    tiles = slice(b * BATCH, (b + 1) * BATCH)
                    pool.wait_ge(nodes_read, BATCHES + b + 1)
                    nc.gpsimd.tensor_tensor(h_nodes[:, tiles, :], h_nodes[:, tiles, :], x_nodes[:, tiles, :], ALU.add).then_inc(nodes_added, 1)
            with pool.If(fast == 1):
                with pool.Fori(0, (FAST - PEEL) // SPAN6) as m:
                    for q in range(SPAN6):
                        gather_group((passes * ITERS + passes + m * SPAN6 + q) * U, q % U, CH, table[:, :])
                for f in range(FAST - PEEL, FAST):
                    gather_group((passes * ITERS + passes + f) * U, f % U, TAIL if f == ITERS else CH, table[:, :])

        @block.scalar
        def _(act):
            load_rows(act, SRC)
            act.wait_ge(params_zeroed, 1)
            nc.scalar.activation(std[:, 0:1], zero[:, :], ACT.Sqrt)
            act.wait_ge(rows_loaded[SRC], 32)
            rows = edge_rows[:, SRC, :, :]
            nc.scalar.copy(rows[:, 0:BLOCKS - 1, :], rows[:, 0:BLOCKS - 1, :].bitcast(i32)).then_inc(rows_are_float[SRC], 1)
            nc.scalar.copy(rows[0:LEFT, BLOCKS - 1, :], rows[0:LEFT, BLOCKS - 1, :].bitcast(i32)).then_inc(rows_are_float[SRC], 1)
            for m, t in enumerate(range(0, BLOCKS, TURN)):
                n = min(TURN * P, CHUNKS - t * P)
                act.wait_ge(rows_turned, m + 1)
                nc.scalar.copy(edges[:, SRC, t * P:t * P + n], turn_ps[m % 2][:, 0:n]).then_inc(sources_ready, 1)
            act.wait_ge(sources_ready, TURNS)
            act.wait_ge(passes_ready, 1)
            passes = act.value_load(n_passes[0:1, 0:1], min_val=1, max_val=EXTRA + 1)

            def index_group(layer, step, g, s, chunks, count, unit=1):
                act.wait_ge(group_summed, slot_is_free(step, unit))
                nc.scalar.copy(idx[:, s, 0:chunks], edges[:, SRC, bass.ds(g * CH, chunks)]).then_inc(idx_ready, count)

            def copy_types(step, chunks, count):
                act.wait_ge(types_turned, step + 1)
                for h in range(-(-chunks // 4)):
                    n = min(4, chunks - 4 * h) * R
                    last = nc.scalar.copy(type_hot_t[0:n, h, :], types_ps[0:n, h * P:h * P + P])
                last.then_inc(types_copied, count)

            def norm_part(layer, part):
                b0, b1, on_act = PARTS[layer][part]
                tiles = slice(b0 * BATCH, b1 * BATCH)
                nodes = h_nodes if layer else x1_new
                act.wait_ge(var_ready, len(PARTS[0]) * layer + part + 1)
                nc.scalar.activation(std[:, tiles], var_eps[:, tiles], ACT.Sqrt).then_inc(std_ready, 1)
                if on_act:
                    act.wait_ge(norm_ready, 1)
                    for t in range(b0 * BATCH, b0 * BATCH + on_act):
                        last = nc.scalar.activation(nodes[:, t, :], nodes[:, t, :], ACT.Identity,
                                                    scale=rstd[:, t:t + 1], bias=neg_mean_rstd[:, t:t + 1])
                    last.then_inc(part_normed[layer][part], 1)

            def begin_block(k, b, r, use):
                act.wait_ge(offsets_ready, k + 1)
                act.wait_ge(blocks_stored[r], (k * BLOCKS_OF[r] + use) * 16 + 16)
                nc.scalar.copy(blocks_out[:, r, :, LEAST:WB], zero[:, 0:1].unsqueeze(2).to_broadcast([P, TILES, WB - LEAST])).then_inc(tail_zeroed, 1)

            def copy_chunk(k, b, r, j):
                n = (k * ITERS + b) * DENSE + j
                offset = act.value_load(offsets[0:1, bass.ds(b, 1), j:j + 1].rearrange("p i j -> p (i j)"), min_val=0, max_val=WB - SPREAD)
                if j == 0:
                    act.wait_ge(tail_zeroed, k * ITERS + b + 1)
                act.wait_ge(dense_summed, n + 1 + FREE_HOTS)
                act.wait_ge(chunk_copied, n + FREE_BANKS)
                nc.scalar.copy(blocks_out[:, r, :, bass.ds(offset, SPREAD)],
                               dense_ps[j % 2][:, 0:KEYS].rearrange("p (h w) -> p h w", h=TILES)).then_inc(chunk_copied, 1)

            with act.Fori(0, passes) as k:
                step0 = k * STEPS
                for s in range(U):
                    index_group(0, step0 + s, s, s, CH, 1)
                act.wait_ge(starts_spread, k + 1)
                for bank, (i0, i1) in zip(START_BANKS, START_ITERS):
                    last = nc.scalar.copy(starts[:, i0:i1, :], bank[:, 0:(i1 - i0) * DENSE].rearrange("p (i j) -> p i j", j=DENSE))
                last.then_inc(starts_copied, 1)
                for s in range(U):
                    copy_types(step0 + s, CH, 1)
                with act.Fori(0, ITERS // 2) as m:
                    for r in range(2):
                        i = m * 2 + (r + 1)
                        for s in range(U):
                            index_group(0, step0 + i * U + s, i * U + s, s, CH, 1)
                            copy_types(step0 + i * U + s, CH, 1)
                            if s == 0:
                                begin_block(k, m * 2 + r, r, m)
                            for j in DENSE_OF[s]:
                                copy_chunk(k, m * 2 + r, r, j)
                index_group(0, step0 + ITERS * U, ITERS * U, 0, TAIL, U)
                copy_types(step0 + ITERS * U, TAIL, U)
                early = load_early(act)
                with act.If(early == 1):
                    norm_part(0, 0)
                begin_block(k, ITERS - 1, 0, ITERS // 2)
                for j in range(DENSE):
                    copy_chunk(k, ITERS - 1, 0, j)
            early = load_early(act)
            with act.If(early == 0):
                norm_part(0, 0)
            norm_part(0, 1)
            slow, fast = load_loops(act)
            with act.If(fast == 0):
                with act.Fori(0, slow) as k:
                    step0 = (k + passes) * STEPS
                    with act.Fori(0, ITERS) as i:
                        for s in range(U):
                            index_group(1, step0 + i * U + s, i * U + s, s, CH, 1)
                    index_group(1, step0 + ITERS * U, ITERS * U, 0, TAIL, U)
                for part in range(len(PARTS[1])):
                    norm_part(1, part)
            with act.If(fast == 1):
                step0 = passes * STEPS
                with act.Fori(0, (FAST - PEEL) // SPAN6) as m:
                    for q in range(SPAN6):
                        f = m * SPAN6 + q
                        index_group(1, step0 + f * U, f * U + (U - 1), q % U, CH, U, U)
                for f in range(FAST - PEEL, ITERS):
                    index_group(1, step0 + f * U, f * U + (U - 1), f % U, CH, U, U)
                    for part, (b0, b1, _) in enumerate(PARTS[1]):
                        if EARLY.get(f - U) == b1 - 1:
                            norm_part(1, part)
                index_group(1, step0 + ITERS * U, ITERS * U, ITERS % U, TAIL, U, U)
                for part, (b0, b1, _) in enumerate(PARTS[1]):
                    if b1 == BATCHES or FAST - 2 * BATCHES + 2 * (b1 - 1) + U >= ITERS:
                        norm_part(1, part)

        @block.tensor
        def _(pe):
            pe.sem_inc(group_summed, FREE)
            pe.sem_inc(dense_summed, FREE_HOTS)
            pe.sem_inc(block_summed, FREE_BANKS)
            pe.wait_ge(consts_ready, 6)
            turned = 0
            for a in (SRC, DST, TYPE, WEIGHT):
                if a == WEIGHT:
                    pe.wait_ge(rows_loaded[a], 32)
                else:
                    pe.wait_ge(rows_are_float[a], 2)
                for t0 in range(0, BLOCKS, TURN):
                    if a == SRC and turned >= 2:
                        pe.wait_ge(sources_ready, turned - 1)
                    elif turned > TURNS + 1:
                        pe.wait_ge(edges_ready, turned - TURNS - 1)
                    for t in range(t0, min(t0 + TURN, BLOCKS)):
                        n = min(P, CHUNKS - t * P)
                        last = nc.tensor.transpose(turn_ps[turned % 2][:, (t - t0) * P:(t - t0) * P + n],
                                                   edge_rows[0:n, a, t, :], ident[0:n, 0:n])
                    last.then_inc(rows_turned, 1)
                    turned += 1
                if a == SRC:
                    pe.wait_ge(diag_ready, 4)
                    for h in range(2):
                        n = P if h == 0 else GROUPS - P
                        nc.tensor.matmul(node_ps[:, P * h:P * h + n], ones[:, :], diag[:, h, 0:n], start=True, stop=True)
                        last = nc.tensor.matmul(node_ps[:, 256 + P * h:256 + P * h + n], ones[:, :], diag[:, 2 + h, 0:n],
                                                start=True, stop=True)
                    last.then_inc(bases_spread, 1)
                    pe.wait_ge(sources_ready, TURNS)
            pe.wait_ge(edges_ready, 3 * TURNS)
            pe.wait_ge(params_loaded, 16 * N_PARAMS)
            pe.wait_ge(passes_ready, 1)
            passes = pe.value_load(n_passes[0:1, 0:1], min_val=1, max_val=EXTRA + 1)

            def turn_types(step, s, chunks, count):
                pe.wait_ge(types_hot, step + 1)
                for h in range(-(-chunks // 4)):
                    n = min(4, chunks - 4 * h)
                    last = nc.tensor.transpose(types_ps[0:n * R, h * P:h * P + P],
                                               type_hot[:, s, 4 * h:4 * h + n, :].rearrange("p c r -> p (c r)"),
                                               ident[:, :])
                last.then_inc(types_turned, count)

            def look_up_coefs(step, s, chunks, count):
                pe.wait_ge(types_copied, step + 1)
                pe.wait_ge(coefs_weighted, step + 1)
                for h in range(-(-chunks // 4)):
                    n = min(4, chunks - 4 * h)
                    last = nc.tensor.matmul(coefs_ps[:, 4 * h * B:(4 * h + n) * B], type_hot_t[0:n * R, h, :],
                                            wc_blocks[0:n * R, 0:n * B], start=True, stop=True)
                last.then_inc(coefs_ready, count)

            def spread_starts(k):
                pe.wait_ge(window_added, k * STEPS + FREE)
                pe.wait_ge(chunk_copied, k * DENSE_CHUNKS + FREE_BANKS)
                for bank, (i0, i1) in zip(START_BANKS, START_ITERS):
                    last = nc.tensor.matmul(bank[:, 0:(i1 - i0) * DENSE].rearrange("p (i j) -> p i j", j=DENSE),
                                            ident[:, 0:1].to_broadcast([P, P]),
                                            edges[:, DST, i0 * U * CH:i1 * U * CH].rearrange("p (i c) -> p i c", c=U * CH)[:, :, 0:DENSE],
                                            start=True, stop=True)
                last.then_inc(starts_spread, 1)

            def sum_chunk(k, b, j):
                n = (k * ITERS + b) * DENSE + j
                pe.wait_ge(hots_ready, n + 1)
                if j == 0:
                    pe.wait_ge(chunk_copied, n + 1)
                for w in range(3):
                    last = nc.tensor.matmul(dense_ps[j % 2][:, 0:KEYS], lo_hot[:, w, j // 2, :, j % 2], node_hot[:, j // 2, :, j % 2],
                                            start=(j == 0 and w == 0), stop=(w == 2), skip_group_check=True)
                last.then_inc(dense_summed, 1)
                if j < DENSE - 1:
                    pe.wait_ge(chunk_copied, n + 2)
                    seam = dense_ps[1 - j % 2][:, 0:KEYS].rearrange("p (h w) -> p h w", h=TILES)[:, :, 0]
                    for w in range(3):
                        nc.tensor.matmul(seam, lo_hot[:, w, j // 2, :, j % 2], carry_hot[:, j // 2, :, j % 2],
                                         start=(w == 0), stop=(w == 2), skip_group_check=True)

            def sum_group(layer, step, s, use, chunks, count, unit=1, beside=None):
                pe.wait_ge(rows_gathered[s], use)
                pe.wait_ge(factors_ready, step + 2)
                pe.wait_ge(window_added, slot_is_free(step, unit))
                for j in range(chunks):
                    if layer == 0:
                        for h in range(2):
                            last = nc.tensor.matmul(sums_ps[s][D * h:D * h + D, 0:HALF * WIN], gathered_rows[:, s, j, 0:D],
                                                    factors[:, s, j, HALF * h:HALF * h + HALF, :].rearrange("p b w -> p (b w)"),
                                                    start=(j == 0), stop=(j == chunks - 1))
                    else:
                        last = nc.tensor.matmul(sums_ps[s][0:D + 1, 0:WIN], gathered_rows[:, s, j, 0:D + 1],
                                                factors[:, s, j, 0, :], start=(j == 0), stop=(j == chunks - 1))
                    if j == chunks - 1:
                        last.then_inc(group_summed, count)
                    if beside and j < len(beside[2]):
                        sum_chunk(beside[0], beside[1], beside[2][j])

            def sum_block(f, r, loads):
                pe.wait_ge(block_loaded[r], loads * 16)
                pe.wait_ge(block_added, f + 1)
                for t in range(TILES):
                    last = nc.tensor.matmul(dense_ps[r][0:D + 1, 0:WB], x1_nodes[:, t, :], blocks_in[:, r, t, :],
                                            start=(t == 0), stop=(t == TILES - 1))
                last.then_inc(block_summed, 1)

            def transform(layer, b, bank):
                for t in range(BATCH):
                    cols = slice((b * BATCH + t) * P, (b * BATCH + t + 1) * P)
                    if layer == 0:
                        to = bank[:, t * D:(t + 1) * D]
                        for c in range(HALF):
                            last = nc.tensor.matmul(to, acc0[:, c, cols], w0_sb[:, c, :], start=(c == 0), stop=(c == HALF - 1))
                    else:
                        last = nc.tensor.matmul(bank[:, t * (D + 1):(t + 1) * (D + 1)], acc1[:, cols], w1_deg[:, :], start=True, stop=True)
                last.then_inc(nodes_out, 1)

            def sum_all(layer, k):
                kk = k + passes if layer else k
                step0 = kk * STEPS
                pe.wait_ge(counts_reset, kk + 1)
                pe.sem_inc(passes_begun, 1)

                def back(i, s, chunks, count, beside=None):
                    sum_group(layer, step0 + i * U + s, s, i * WHOLE + 16 * chunks, chunks, count, 1, beside)

                if layer == 1:
                    for s in range(U):
                        back(0, s, CH, 1)
                    with pe.Fori(1, ITERS) as i:
                        for s in range(U):
                            back(i, s, CH, 1)
                    back(ITERS, 0, TAIL, U)
                    return

                def turn(i, s, chunks, count):
                    turn_types(step0 + i * U + s, s, chunks, count)

                def look_up(i, s, chunks, count):
                    look_up_coefs(step0 + i * U + s, s, chunks, count)

                spread_starts(k)
                for s in range(U):
                    turn(0, s, CH, 1)
                    if s == 2:
                        back(0, 0, CH, 1)
                    look_up(0, s, CH, 1)
                def step(i, s):
                    turn(i, s, CH, 1)
                    if s < 2:
                        back(i - 1, s + 1, CH, 1, (k, i - 1, DENSE_OF[s]))
                    else:
                        back(i, 0, CH, 1, (k, i - 1, DENSE_OF[s]))
                    look_up(i, s, CH, 1)

                with pe.Fori(1, FIRST_EARLY) as i:
                    for s in range(U):
                        step(i, s)
                early = load_early(pe)

                def early_is_read(b):
                    with pe.If(early == 1):
                        pe.wait_ge(nodes_read, b + 1)

                for i in range(FIRST_EARLY, ITERS):
                    for s in range(U):
                        b = (i - FIRST_EARLY) * 2 + s
                        if s == 0 and b > 0:
                            early_is_read(b - 1)
                        elif s == 2:
                            early_is_read(b - 2)
                        step(i, s)
                        if s < 2:
                            with pe.If(early == 1):
                                pe.wait_ge(window_added, step0 + (i - 1) * U + s + 1 + FREE)
                                transform(0, b, sums_ps[s])
                turn(ITERS, 0, TAIL, U)
                early_is_read(BATCHES - 2)
                back(ITERS - 1, 1, CH, 1, (k, ITERS - 1, range(0, CH)))
                look_up(ITERS, 0, TAIL, U)
                back(ITERS - 1, 2, CH, 1, (k, ITERS - 1, range(CH, DENSE)))
                back(ITERS, 0, TAIL, U)

            with pe.Fori(0, passes) as k:
                sum_all(0, k)
            pe.wait_ge(checked, passes)
            nc.tensor.matmul(types_ps[:, 0:1], ones[:, :], n_broken[:, :], start=True, stop=True).then_inc(broken_counted, 1)
            early = load_early(pe)
            pe.wait_ge(window_added, passes * STEPS + FREE)
            with pe.If(early == 0):
                for b in range(BATCHES - 1):
                    if b >= U:
                        pe.wait_ge(nodes_read, b - U + 1)
                    transform(0, b, sums_ps[b % U])
            pe.wait_ge(nodes_read, BATCHES - U)
            transform(0, BATCHES - 1, sums_ps[(BATCHES - 1) % U])
            pe.wait_ge(nodes_read, BATCHES)
            pe.wait_ge(x1_copied, 1)
            for t in range(TILES):
                if t % 4 == 0 and t // 4 >= len(self_ps):
                    pe.wait_ge(self_added, t // 4 - len(self_ps) + 1)
                last = nc.tensor.transpose(self_ps[t // 4 % len(self_ps)][0:D + 1, (t % 4) * P:(t % 4 + 1) * P], x1_nodes[:, t, :], ident[:, :])
                if t % 4 == 3 or t == TILES - 1:
                    last.then_inc(x1_turned, 1)
            slow, fast = load_loops(pe)
            pe.wait_ge(self_added, -(-TILES // 4))
            with pe.If(fast == 0):
                with pe.Fori(0, slow) as k:
                    sum_all(1, k)
                pe.wait_ge(window_added, passes * 2 * STEPS + FREE)
                for b in range(BATCHES):
                    if b >= U:
                        pe.wait_ge(nodes_read, BATCHES + b - U + 1)
                    transform(1, b, sums_ps[b % U])
            with pe.If(fast == 1):
                step0 = passes * STEPS
                use0 = PER_PASS

                def transform_early(f, b):
                    pe.wait_ge(window_added, step0 + f * U + FREE)
                    pe.wait_ge(block_added, min(f, ITERS) + FREE_BANKS)
                    if b >= len(early_ps):
                        pe.wait_ge(nodes_read, BATCHES + b - len(early_ps) + 1)
                    transform(1, b, early_ps[b % len(early_ps)])

                with pe.Fori(0, (FAST - PEEL) // SPAN6) as m:
                    for q in range(SPAN6):
                        f = m * SPAN6 + q
                        sum_block(f, q % 2, m * (SPAN6 // 2) + (q // 2 + 1))
                        sum_group(1, step0 + f * U, q % U, use0[q % U] + m * (SPAN6 // U * WHOLE) + (q // U + 1) * WHOLE, CH, U, U)
                for f in range(FAST - PEEL, ITERS):
                    if f < ITERS - 1:
                        sum_block(f, f % 2, f // 2 + 1)
                    if f == ITERS - 2:
                        sum_block(f + 1, (f + 1) % 2, (f + 1) // 2 + 1)
                    if f in EARLY:
                        transform_early(f, EARLY[f])
                    sum_group(1, step0 + f * U, f % U, use0[f % U] + (f // U + 1) * WHOLE, CH, U, U)
                sum_group(1, step0 + ITERS * U, ITERS % U, use0[ITERS % U] + ITERS // U * WHOLE + 16 * TAIL, TAIL, U, U)
                transform_early(FAST, BATCHES - 1)

        @block.vector
        def _(dve):
            nc.vector.memset(room[:, 4 * BLOCKS * P:2 * BLK], 0.0)
            nc.vector.memset(edge_rows[:, :, BLOCKS - 1, :], 0.0).then_inc(room_zeroed, 1)
            nc.vector.memset(x_nodes[:, TILES - 1, :], 0.0)
            nc.vector.memset(wc_blocks[:, :], 0.0)
            nc.vector.memset(zero[:, :], 0.0)
            nc.vector.memset(w1_deg[0:D, D:D + 1], 0.0)
            nc.vector.memset(w1_deg[D:D + 1, 0:D], 0.0)
            nc.vector.memset(w1_deg[D:D + 1, D:D + 1], 1.0).then_inc(params_zeroed, 1)
            dve.sem_inc(window_added, FREE)
            dve.sem_inc(chunk_copied, FREE_BANKS)
            dve.sem_inc(block_added, FREE_BANKS)
            dve.sem_inc(coefs_weighted, 1)
            dve.sem_inc(factors_ready, 1)

            nc.vector.memset(lo[:, 1:2], 0.0).then_inc(start_step, 1)
            nc.vector.memset(hi[:, 1:2], 0.0).then_inc(start_step, 1)
            dve.wait_ge(start_step, 2)
            dve.wait_ge(dst_loaded, 48)
            for h in range(2):
                n = P if h == 0 else GROUPS - P
                nc.vector.tensor_reduce(lo[0:n, h:h + 1], dst_by_group[0:n, h, :], AX.X, ALU.min).then_inc(start_step, 1)
                nc.vector.tensor_reduce(hi[0:n, h:h + 1], dst_by_group[0:n, h, :], AX.X, ALU.max).then_inc(start_step, 1)
            dve.wait_ge(start_step, 6)
            nc.vector.tensor_tensor(span[:, :], hi[:, :], lo[:, :], ALU.subtract).then_inc(start_step, 1)
            dve.wait_ge(start_step, 7)
            dve.wait_ge(consts_ready, 6)
            for h in range(2):
                nc.vector.tensor_scalar(diag[:, h, :], ident[:, :], lo[:, h:h + 1], None, ALU.mult).then_inc(diag_ready, 1)
                nc.vector.tensor_scalar(diag[:, 2 + h, :], ident[:, :], span[:, h:h + 1], None, ALU.mult).then_inc(diag_ready, 1)
            nc.vector.tensor_copy(type_iota, type_iota_sb[:, :])
            nc.vector.tensor_copy(key_iota[:, :, :], key_iota_f)
            nc.vector.memset(hi_key[:, :, DENSE - 1:DENSE], -1.0)
            nc.vector.tensor_copy(win_iota, win_iota_sb[:, :]).then_inc(start_step, 1)
            dve.wait_ge(bases_spread, 1)
            nc.vector.tensor_reduce(max_span[:, :], node_ps[:, 256:256 + GROUPS], AX.X, ALU.max).then_inc(start_step, 1)
            dve.wait_ge(start_step, 9)
            nc.vector.tensor_scalar(further, win_steps, max_span[:, 0:1], None, ALU.is_le).then_inc(start_step, 1)
            dve.wait_ge(start_step, 10)
            nc.vector.tensor_reduce(n_further[:, :], further, AX.X, ALU.add).then_inc(start_step, 1)
            dve.wait_ge(start_step, 11)
            nc.vector.tensor_scalar(n_passes[0:1, :], n_further[0:1, :], 1.0, None, ALU.add).then_inc(passes_ready, 1)
            nc.vector.tensor_copy(first_base[:, :], node_ps[:, 0:GROUPS]).then_inc(start_step, 1)
            for a in (DST, TYPE):
                dve.wait_ge(rows_loaded[a], 32)
                rows = edge_rows[:, a, :, :]
                nc.vector.tensor_copy(rows[:, 0:BLOCKS - 1, :], rows[:, 0:BLOCKS - 1, :].bitcast(i32)).then_inc(rows_are_float[a], 1)
                nc.vector.tensor_copy(rows[0:LEFT, BLOCKS - 1, :], rows[0:LEFT, BLOCKS - 1, :].bitcast(i32)).then_inc(rows_are_float[a], 1)
            turned = TURNS
            for a in (DST, TYPE, WEIGHT):
                for t in range(0, BLOCKS, TURN):
                    n = min(TURN * P, CHUNKS - t * P)
                    dve.wait_ge(rows_turned, turned + 1)
                    nc.vector.tensor_copy(edges[:, a, t * P:t * P + n], turn_ps[turned % 2][:, 0:n]).then_inc(edges_ready, 1)
                    turned += 1
            dve.wait_ge(params_loaded, 16 * N_PARAMS)
            nc.vector.tensor_scalar(neg_bias0[:, :], bias0_bc[:, :], -1.0, None, ALU.mult).then_inc(bias_ready, 1)
            dve.wait_ge(edges_ready, 3 * TURNS)
            dve.wait_ge(bias_ready, 1)
            dve.wait_ge(start_step, 12)
            dve.wait_ge(acc_zeroed, 1)
            dve.wait_ge(passes_ready, 1)
            passes = dve.value_load(n_passes[0:1, 0:1], min_val=1, max_val=EXTRA + 1)

            def take_starts(k):
                dve.wait_ge(starts_copied, k + 1)
                dve.wait_ge(chunk_copied, k * DENSE_CHUNKS + FREE_BANKS)
                nc.vector.tensor_tensor(start_room, starts[0:1, :, :], starts[0:1, :, 0:1].to_broadcast([1, ITERS, DENSE]),
                                        ALU.subtract).then_inc(starts_ready, 1)
                dve.wait_ge(starts_ready, k + 1)
                nc.vector.tensor_scalar(offsets[:, :, :], start_room, 0.0, float(WB - SPREAD), ALU.max, ALU.min).then_inc(offsets_ready, 1)
                nc.vector.memset(greatest[:, :], -float(P * P * P))
                nc.vector.memset(least[:, :], float(P * P * P)).then_inc(key_step, 1)

            def make_keys(k, piece, first, n):
                its = bass.ds(first, n)
                of_chunks = edges[:, :, bass.ds(first * (U * CH), n * U * CH)].rearrange("p a (i c) -> p a i c", c=U * CH)
                sources, dests, weights = (of_chunks[:, a, :, 0:DENSE] for a in (SRC, DST, WEIGHT))
                begin = starts[:, its, :]
                hi, rest, at_node = (key_room[q][:, 0:n, :] for q in range(3))
                to_next = at_node[:, :, 1:DENSE]
                done = (k * KEY_PIECES + piece) * KEY_STEPS + (k + 1)
                at = [0]

                def step(instruction):
                    at[0] += 1
                    instruction.then_inc(key_step, 1)
                    dve.wait_ge(key_step, done + at[0])

                dve.wait_ge(key_step, done)
                step(nc.vector.tensor_scalar(rest, sources, 1.0 / P, -(P - 1) / (2.0 * P), ALU.mult, ALU.add))
                step(nc.vector.tensor_scalar(rest, rest, ROUND, None, ALU.add))
                step(nc.vector.tensor_scalar(hi, rest, ROUND, None, ALU.subtract))
                nc.vector.scalar_tensor_tensor(lo_key[:, its, :], hi, -float(P), sources, ALU.mult, ALU.add)
                step(nc.vector.tensor_tensor(at_node, dests, begin, ALU.subtract))
                nc.vector.tensor_reduce(found[:, 0:1], at_node, AX.XY, ALU.max)
                nc.vector.tensor_reduce(found[:, 3:4], at_node, AX.XY, ALU.min)
                step(nc.vector.scalar_tensor_tensor(node_key[:, its, :], hi, float(SPREAD), at_node, ALU.mult, ALU.add))
                step(nc.vector.tensor_tensor(to_next, begin[:, :, 1:DENSE], dests[:, :, 0:DENSE - 1], ALU.subtract))
                nc.vector.tensor_reduce(found[:, 1:2], to_next, AX.XY, ALU.max)
                nc.vector.tensor_reduce(found[:, 4:5], to_next, AX.XY, ALU.min)
                step(nc.vector.scalar_tensor_tensor(hi_key[:, its, 0:DENSE - 1], to_next, -float(P), hi[:, :, 0:DENSE - 1], ALU.mult, ALU.add))
                nc.vector.tensor_tensor(to_next, begin[:, :, 1:DENSE], begin[:, :, 0:DENSE - 1], ALU.subtract)
                step(nc.vector.tensor_tensor(at_node[:, :, 0], begin[:, :, DENSE - 1], begin[:, :, 0], ALU.subtract))
                nc.vector.tensor_reduce(found[:, 5:6], to_next, AX.XY, ALU.min)
                nc.vector.tensor_reduce(found[:, 2:3], at_node[:, :, 0], AX.X, ALU.max)
                nc.vector.tensor_reduce(found[:, 6:7], at_node[:, :, 0], AX.X, ALU.min)
                step(nc.vector.tensor_scalar(w_part[0][:, its, :], weights, 1.0, None, ALU.mult))
                step(nc.vector.tensor_tensor(rest, weights, w_part[0][:, its, :], ALU.subtract))
                step(nc.vector.tensor_scalar(w_part[1][:, its, :], rest, 1.0, None, ALU.mult))
                nc.vector.tensor_tensor(w_part[2][:, its, :], rest, w_part[1][:, its, :], ALU.subtract)
                nc.vector.tensor_tensor(greatest[:, :], greatest[:, :], found[:, 0:3], ALU.max)
                step(nc.vector.tensor_tensor(least[:, :], least[:, :], found[:, 3:7], ALU.min))
                assert at[0] == KEY_STEPS

            def check_keys():
                for c, most in enumerate((SPREAD - 1, SPREAD, WB - SPREAD)):
                    nc.vector.tensor_scalar(broken[:, c:c + 1], greatest[:, c:c + 1], float(most), None, ALU.is_gt)
                for c, fewest in enumerate((0, 0, 1, LEAST - SPREAD)):
                    last = nc.vector.tensor_scalar(broken[:, 3 + c:4 + c], least[:, c:c + 1], float(fewest), None, ALU.is_lt)
                last.then_inc(keys_checked, 1)

            def make_hots(k, b, js):
                j0, j1 = js[0], js[-1] + 1
                q0, q1 = j0 // 2, j1 // 2
                n = (k * ITERS + b) * DENSE

                def compared(values):
                    return key_iota[:, 0:values, :].unsqueeze(1).to_broadcast([P, q1 - q0, values, 2])

                def keys(array, values):
                    of_pairs = array[:, bass.ds(b, 1), j0:j1].rearrange("p i (q t) -> p (i q) t", t=2)
                    return of_pairs.unsqueeze(2).to_broadcast([P, q1 - q0, values, 2])

                dve.wait_ge(dense_summed, n + min(j1 + 1, DENSE))
                nc.vector.tensor_tensor(lo_hot[:, 2, q0:q1, :, :], compared(P), keys(lo_key, P), ALU.is_equal).then_inc(lo_hots_ready, 1)
                nc.vector.tensor_tensor(carry_hot[:, q0:q1, :, :], compared(TILES), keys(hi_key, TILES), ALU.is_equal)
                nc.vector.tensor_tensor(node_hot[:, q0:q1, :, :], compared(KEYS), keys(node_key, KEYS), ALU.is_equal)
                dve.wait_ge(lo_hots_ready, (k * ITERS + b) * U + (DENSE_OF.index(js) + 1))
                for w in range(3):
                    last = nc.vector.tensor_tensor(lo_hot[:, w, q0:q1, :, :], lo_hot[:, 2, q0:q1, :, :], keys(w_part[w], P), ALU.mult)
                last.then_inc(hots_ready, len(js))

            def compare_types(step, g, s, chunks, count):
                cols = bass.ds(g * CH, chunks)
                nc.vector.tensor_tensor(type_hot[:, s, 0:chunks, :],
                                        edges[:, TYPE, cols].unsqueeze(2).to_broadcast([P, chunks, R]),
                                        type_iota.unsqueeze(1).to_broadcast([P, chunks, R]),
                                        ALU.is_equal).then_inc(types_hot, count)

            def weigh(layer, step, g, s, chunks, count, unit=1):
                cols = bass.ds(g * CH, chunks)
                dve.wait_ge(factors_ready, step + 1)
                nc.vector.tensor_tensor(hits[:, 0:chunks, :], win_iota.unsqueeze(1).to_broadcast([P, chunks, WIN]),
                                        local_dst[:, cols].unsqueeze(2).to_broadcast([P, chunks, WIN]),
                                        ALU.is_equal).then_inc(hits_ready, count)
                dve.wait_ge(group_summed, slot_is_free(step, unit))
                if layer == 0:
                    dve.wait_ge(coefs_ready, step + 1)
                    nc.vector.tensor_tensor(coef_w[:, s, 0:chunks, :],
                                            coefs_ps[:, 0:chunks * B].rearrange("p (c b) -> p c b", b=B),
                                            edges[:, WEIGHT, cols].unsqueeze(2).to_broadcast([P, chunks, B]),
                                            ALU.mult).then_inc(coefs_weighted, count)
                    dve.wait_ge(coefs_weighted, step + 2)
                    dve.wait_ge(hits_ready, step + 1)
                    nc.vector.tensor_tensor(factors[:, s, 0:chunks, :, :],
                                            hits[:, 0:chunks, :].unsqueeze(2).to_broadcast([P, chunks, B, WIN]),
                                            coef_w[:, s, 0:chunks, :].unsqueeze(3).to_broadcast([P, chunks, B, WIN]),
                                            ALU.mult).then_inc(factors_ready, count)
                else:
                    dve.wait_ge(hits_ready, step + 1)
                    nc.vector.tensor_tensor(factors[:, s, 0:chunks, 0, :], hits[:, 0:chunks, :],
                                            edges[:, WEIGHT, cols].unsqueeze(2).to_broadcast([P, chunks, WIN]),
                                            ALU.mult).then_inc(factors_ready, count)

            def add_window(layer, step, g, s, count, blocks=None):
                node = dve.value_load(base_int[0:1, bass.ds(g, 1)], min_val=0, max_val=N)
                dve.wait_ge(group_summed, step + 1 + FREE)
                dve.wait_ge(window_added, step + FREE)
                if blocks is not None:
                    dve.wait_ge(block_added, blocks + FREE_BANKS)
                if layer == 0:
                    nc.vector.tensor_tensor(acc0[:, :, bass.ds(node, WIN)], acc0[:, :, bass.ds(node, WIN)],
                                            sums_ps[s][:, 0:HALF * WIN].rearrange("p (b w) -> p b w", b=HALF),
                                            ALU.add).then_inc(window_added, count)
                else:
                    nc.vector.tensor_tensor(acc1[:, bass.ds(node, WIN)], acc1[:, bass.ds(node, WIN)],
                                            sums_ps[s][0:D + 1, 0:WIN], ALU.add).then_inc(window_added, count)

            def first_windows():
                whole = (GROUPS - 1) * CH
                nc.vector.tensor_copy(base[:, :], first_base[0:1, :]).then_inc(base_ready, 1)
                nc.vector.tensor_copy(base_int[:, :], first_base[0:1, :]).then_inc(base_ready, 1)
                nc.vector.tensor_tensor(local_dst[:, 0:whole].rearrange("p (g c) -> p g c", c=CH),
                                        edges[:, DST, 0:whole].rearrange("p (g c) -> p g c", c=CH),
                                        first_base[:, 0:GROUPS - 1].unsqueeze(2).to_broadcast([P, GROUPS - 1, CH]),
                                        ALU.subtract).then_inc(base_ready, 1)
                nc.vector.tensor_tensor(local_dst[:, whole:CHUNKS], edges[:, DST, whole:CHUNKS],
                                        first_base[:, GROUPS - 1:GROUPS].to_broadcast([P, TAIL]),
                                        ALU.subtract).then_inc(base_ready, 1)

            def norm_step_of(layer, part):
                done = sum(norm_steps(l, p) for l in range(2) for p in range(len(PARTS[l])) if (l, p) < (layer, part))

                def step(instruction, n, wait=True):
                    instruction.then_inc(norm_step, 1)
                    if wait:
                        dve.wait_ge(norm_step, done + n)

                return step

            def begin_norm(layer, part):
                b0, b1, _ = PARTS[layer][part]
                ts = slice(b0 * BATCH, b1 * BATCH)
                step = norm_step_of(layer, part)
                dve.wait_ge(stats_ready, BATCHES * layer + b1)
                step(nc.vector.tensor_tensor(half_diff[:, ts], stats[:, ts, 1], stats[:, ts, 4], ALU.subtract), 1, False)
                step(nc.vector.tensor_tensor(var_eps[:, ts], stats[:, ts, 2], stats[:, ts, 5], ALU.add), 2, False)
                step(nc.vector.tensor_tensor(mean[:, ts], stats[:, ts, 1], stats[:, ts, 4], ALU.add), 3)
                step(nc.vector.scalar_tensor_tensor(half_diff[:, ts], half_diff[:, ts], 0.25, half_diff[:, ts], ALU.mult, ALU.mult), 4, False)
                step(nc.vector.tensor_scalar(var_eps[:, ts], var_eps[:, ts], 1.0 / D, EPS, ALU.mult, ALU.add), 5, False)
                step(nc.vector.tensor_scalar(mean[:, ts], mean[:, ts], 0.5, None, ALU.mult), 6)
                nc.vector.tensor_tensor(var_eps[:, ts], var_eps[:, ts], half_diff[:, ts], ALU.add).then_inc(var_ready, 1)

            def end_norm(layer, part):
                step = norm_step_of(layer, part)
                b0, b1, on_act = PARTS[layer][part]
                ts = slice(b0 * BATCH, b1 * BATCH)
                nodes = h_nodes if layer else x1_new
                dve.wait_ge(std_ready, len(PARTS[0]) * layer + part + 1)
                step(nc.vector.reciprocal(rstd[:, ts], std[:, ts]), 7)
                step(nc.vector.tensor_tensor(newton[:, ts], rstd[:, ts], rstd[:, ts], ALU.mult), 8)
                step(nc.vector.scalar_tensor_tensor(newton[:, ts], newton[:, ts], -0.5, var_eps[:, ts], ALU.mult, ALU.mult), 9)
                step(nc.vector.scalar_tensor_tensor(rstd[:, ts], newton[:, ts], 1.5, rstd[:, ts], ALU.add, ALU.mult), 10)
                if on_act:
                    step(nc.vector.scalar_tensor_tensor(neg_mean_rstd[:, ts], mean[:, ts], -1.0, rstd[:, ts], ALU.mult, ALU.mult), 11)
                    dve.sem_inc(norm_ready, 1)
                t0, t1 = b0 * BATCH + on_act, b1 * BATCH
                if (layer, part) == (0, 0):
                    dve.sem_inc(rstd_ready, 1)
                    t1 = POOL_NORMS[0]
                ts, n = slice(t0, t1), t1 - t0
                step(nc.vector.tensor_tensor(nodes[:, ts, :], nodes[:, ts, :], mean[:, ts].unsqueeze(2).to_broadcast([P, n, D]), ALU.subtract),
                     norm_steps(layer, part))
                nc.vector.tensor_tensor(nodes[:, ts, :], nodes[:, ts, :], rstd[:, ts].unsqueeze(2).to_broadcast([P, n, D]),
                                        ALU.mult).then_inc(part_normed[layer][part], 1)

            def norm_part(layer, part):
                begin_norm(layer, part)
                end_norm(layer, part)

            def count_loops():
                dve.wait_ge(broken_counted, 1)
                nc.vector.tensor_tensor(not_fast[:, :], types_ps[0:1, 0:1], n_further[0:1, :], ALU.add).then_inc(loop_step, 1)
                dve.wait_ge(loop_step, 1)
                nc.vector.tensor_scalar(not_fast[:, :], not_fast[:, :], 0.0, None, ALU.is_gt).then_inc(loop_step, 1)
                dve.wait_ge(loop_step, 2)
                nc.vector.scalar_tensor_tensor(loops[:, 0:1], n_further[0:1, :], 1.0, not_fast[:, :], ALU.add, ALU.mult)
                nc.vector.tensor_scalar(loops[:, 1:2], not_fast[:, :], -1.0, 1.0, ALU.mult, ALU.add).then_inc(loops_ready, 1)

            def take_x1(b, bank):
                tiles = slice(b * BATCH, (b + 1) * BATCH)
                dve.wait_ge(nodes_out, b + 1)
                rows = bank[:, 0:BATCH * D].rearrange("p (t f) -> p t f", t=BATCH)
                nc.vector.tensor_tensor(x1_new[:, tiles, :], rows, neg_bias0[:, :].unsqueeze(1).to_broadcast([P, BATCH, D]),
                                        ALU.max).then_inc(nodes_read, 1)
                dve.wait_ge(nodes_read, b + 1)
                nc.vector.tensor_tensor(x1_new[:, tiles, :], x1_new[:, tiles, :], bias0_bc[:, :].unsqueeze(1).to_broadcast([P, BATCH, D]),
                                        ALU.add).then_inc(x1_step, 1)
                dve.wait_ge(x_loaded, 32)
                dve.wait_ge(x1_step, 2 * b + 1)
                nc.vector.tensor_tensor(x1_new[:, tiles, :], x1_new[:, tiles, :], x_nodes[:, tiles, :], ALU.add).then_inc(x1_step, 1)
                dve.wait_ge(x1_step, 2 * b + 2)
                for t in range(b * BATCH, (b + 1) * BATCH):
                    taken = nc.vector.bn_stats(stats[:, t, :], x1_new[:, t, :])
                taken.then_inc(stats_ready, 1)

            def read_nodes(b, bank, stats_of=None):
                stats_left = list(range(stats_of * BATCH, stats_of * BATCH + BATCH)) if stats_of is not None else []
                if stats_left:
                    dve.wait_ge(nodes_added, stats_of + 1)

                def take_stats(n):
                    for _ in range(min(n, len(stats_left))):
                        t = stats_left.pop(0)
                        taken = nc.vector.bn_stats(stats[:, t, :], h_nodes[:, t, :])
                        if not stats_left:
                            taken.then_inc(stats_ready, 1)

                if b == BATCHES:
                    take_stats(BATCH)
                    return
                tiles = slice(b * BATCH, (b + 1) * BATCH)
                dve.wait_ge(nodes_out, BATCHES + b + 1)
                rows = bank[:, 0:BATCH * (D + 1)].rearrange("p (t f) -> p t f", t=BATCH)
                nc.vector.tensor_scalar(has_deg[:, tiles], rows[:, :, D], 0.0, None, ALU.is_gt)
                nc.vector.tensor_scalar(inv_deg[:, tiles], rows[:, :, D], TINY, None, ALU.max).then_inc(deg_step, 1)
                take_stats(2)
                dve.wait_ge(deg_step, 3 * b + 1)
                nc.vector.reciprocal(inv_deg[:, tiles], inv_deg[:, tiles]).then_inc(deg_step, 1)
                take_stats(2)
                dve.wait_ge(deg_step, 3 * b + 2)
                nc.vector.tensor_tensor(inv_deg[:, tiles], inv_deg[:, tiles], has_deg[:, tiles], ALU.mult).then_inc(deg_step, 1)
                take_stats(2)
                dve.wait_ge(deg_step, 3 * b + 3)
                nc.vector.tensor_tensor(h_nodes[:, tiles, :], rows[:, :, 0:D], inv_deg[:, tiles].unsqueeze(2).to_broadcast([P, BATCH, D]),
                                        ALU.mult).then_inc(nodes_read, 1)
                take_stats(BATCH)

            def find_early():
                for b in range(BATCHES - 1):
                    left = (FIRST_EARLY + b // 2 - 1) * U + b % 2 + 1
                    last = nc.vector.tensor_reduce(least_behind[:, b:b + 1], first_base[0:1, left:GROUPS], AX.X, ALU.min)
                last.then_inc(early_step, 1)
                dve.wait_ge(early_step, 1)
                for b in range(BATCHES - 1):
                    last = nc.vector.tensor_scalar(reached[:, b:b + 1], least_behind[:, b:b + 1], float((b + 1) * BATCH * P), None, ALU.is_lt)
                last.then_inc(early_step, 1)
                dve.wait_ge(early_step, 2)
                nc.vector.tensor_reduce(not_early[:, :], reached[:, :], AX.X, ALU.add).then_inc(early_step, 1)
                dve.wait_ge(early_step, 3)
                nc.vector.tensor_tensor(not_early[:, :], not_early[:, :], n_further[0:1, :], ALU.add).then_inc(early_step, 1)
                dve.wait_ge(early_step, 4)
                nc.vector.tensor_scalar(not_early[:, :], not_early[:, :], 0.0, None, ALU.is_gt).then_inc(early_step, 1)
                dve.wait_ge(early_step, 5)
                nc.vector.tensor_scalar(early_flag[:, :], not_early[:, :], -1.0, 1.0, ALU.mult, ALU.add).then_inc(early_ready, 1)

            def check_early():
                for f, b in EARLY.items():
                    last = nc.vector.tensor_reduce(least_left[:, b:b + 1], first_base[:, f * U:GROUPS], AX.X, ALU.min)
                last.then_inc(least_left_found, 1)
                dve.wait_ge(least_left_found, 1)
                for b in EARLY.values():
                    last = nc.vector.tensor_scalar(broken[:, 7 + b:8 + b], least_left[:, b:b + 1], float((b + 1) * BATCH * P), None, ALU.is_lt)
                last.then_inc(least_left_found, 1)

            def weigh_all(layer, k):
                kk = k + passes if layer else k
                step0 = kk * STEPS
                dve.wait_ge(base_ready, kk * 3 + 4 + 4 * layer)

                def types(i, s, chunks, count):
                    compare_types(step0 + i * U + s, i * U + s, s, chunks, count)

                def front(i, s, chunks, count):
                    weigh(layer, step0 + i * U + s, i * U + s, s, chunks, count)

                def back(i, s, count):
                    add_window(layer, step0 + i * U + s, i * U + s, s, count)

                def hots(b, s):
                    make_hots(k, b, DENSE_OF[s])

                def iteration(i, piece=None, early=None):
                    for s in range(U):
                        types(i, s, CH, 1)
                        if s == 0:
                            front(i - 1, U - 1, CH, 1)
                        else:
                            front(i, s - 1, CH, 1)
                        back(i - 1, s, 1)
                        if s == 1 and piece:
                            make_keys(k, *piece)
                        hots(i - 1 if s < U - 1 else i, (s + 1) % U)
                        if early is not None and s > 0:
                            with dve.If(early == 1):
                                take_x1((i - FIRST_EARLY) * 2 + s - 1, sums_ps[s - 1])
                                if i == ITERS - 1 and s == U - 1:
                                    begin_norm(0, 0)

                def move_windows():
                    nc.vector.tensor_scalar(base[:, :], base[:, :], float(WIN), float(N), ALU.add, ALU.min).then_inc(base_ready, 1)
                    nc.vector.tensor_scalar(local_dst[:, :], local_dst[:, :], float(WIN), None, ALU.subtract).then_inc(base_ready, 1)

                if layer == 1:
                    for s in range(U):
                        front(0, s, CH, 1)
                        back(0, s, 1)
                    with dve.Fori(1, ITERS) as i:
                        for s in range(U):
                            front(i, s, CH, 1)
                            back(i, s, 1)
                    front(ITERS, 0, TAIL, U)
                    move_windows()
                    back(ITERS, 0, U)
                else:
                    for s in range(U):
                        types(0, s, CH, 1)
                        if s == 1:
                            dve.wait_ge(dense_summed, k * DENSE_CHUNKS + FREE_HOTS)
                            take_starts(k)
                        if s > 0:
                            front(0, s - 1, CH, 1)
                    make_keys(k, 0, 0, 1)
                    hots(0, 0)
                    iteration(1, (1, 1, FIRST_KEYS - 1))
                    with dve.Fori(2, KEY_PIECES) as i:
                        iteration(i, (i, i * KEY_PIECE + (FIRST_KEYS - 2 * KEY_PIECE), KEY_PIECE))
                    with dve.If(k == 0):
                        find_early()
                        check_early()
                    with dve.Fori(KEY_PIECES, FIRST_EARLY) as i:
                        iteration(i)
                    early = load_early(dve)
                    for i in range(FIRST_EARLY, ITERS):
                        iteration(i, None, early)
                    types(ITERS, 0, TAIL, U)
                    front(ITERS - 1, 2, CH, 1)
                    back(ITERS - 1, 0, 1)
                    hots(ITERS - 1, 1)
                    hots(ITERS - 1, 2)
                    front(ITERS, 0, TAIL, U)
                    with dve.If(early == 1):
                        end_norm(0, 0)
                    check_keys()
                    move_windows()
                    dve.wait_ge(keys_checked, k + 1)
                    dve.wait_ge(least_left_found, 2)
                    nc.vector.tensor_reduce(n_broken[:, :], broken[:, :], AX.X, ALU.add).then_inc(checked, 1)
                    back(ITERS - 1, 1, 1)
                    back(ITERS - 1, 2, 1)
                    back(ITERS, 0, U)
                dve.wait_ge(window_added, step0 + STEPS + FREE)
                dve.wait_ge(base_ready, kk * 3 + 6 + 4 * layer)
                nc.vector.tensor_copy(base_int[:, :], base[:, :]).then_inc(base_ready, 1)

            def add_block(f, r, step):
                node = dve.value_load(base_int[0:1, bass.ds(f * U, 1)], min_val=0, max_val=N)
                dve.wait_ge(block_summed, f + 1 + FREE_BANKS)
                dve.wait_ge(window_added, step + FREE)
                nc.vector.tensor_tensor(acc1[:, bass.ds(node, WB)], acc1[:, bass.ds(node, WB)],
                                        dense_ps[r][0:D + 1, 0:WB], ALU.add).then_inc(block_added, 1)

            first_windows()
            with dve.Fori(0, passes) as k:
                weigh_all(0, k)
            early = load_early(dve)
            with dve.If(early == 0):
                for b in range(BATCHES - 1):
                    take_x1(b, sums_ps[b % U])
                norm_part(0, 0)
            count_loops()
            take_x1(BATCHES - 1, sums_ps[(BATCHES - 1) % U])
            norm_part(0, 1)
            for r in range(2):
                dve.wait_ge(blocks_stored[r], passes * BLOCKS_OF[r] * 16 + 16)
            nc.vector.memset(x1_nodes[:, :, D:D + 1], 1.0)
            for part in range(len(PARTS[0])):
                dve.wait_ge(x1_normed[part], norm_shares(0, part))
            nc.vector.tensor_copy(x1_nodes[:, :, 0:D], x1_new[:, :, :]).then_inc(x1_copied, 1)
            dve.wait_ge(base_ready, passes * 3 + 4)
            first_windows()
            dve.wait_ge(base_ready, passes * 3 + 8)
            for q in range(-(-TILES // 4)):
                n = min(4, TILES - 4 * q) * P
                dve.wait_ge(x1_turned, q + 1)
                nc.vector.tensor_copy(acc1[:, q * 4 * P:q * 4 * P + n], self_ps[q % len(self_ps)][0:D + 1, 0:n]).then_inc(self_added, 1)
            dve.wait_ge(self_added, -(-TILES // 4))
            dve.wait_ge(x1_copied, 1)
            nc.vector.tensor_tensor(x_nodes[:, :, :], x1_nodes[:, :, 0:D], bias1_bc[:, :].unsqueeze(1).to_broadcast([P, TILES, D]),
                                    ALU.add).then_inc(bias_added, 1)
            slow, fast = load_loops(dve)
            with dve.If(fast == 0):
                with dve.Fori(0, slow) as k:
                    weigh_all(1, k)
                for b in range(BATCHES + 2):
                    read_nodes(min(b, BATCHES), sums_ps[b % U], b - 2 if b >= 2 else None)
                    for part, (b0, b1, _) in enumerate(PARTS[1]):
                        if b - 1 == b1:
                            norm_part(1, part)
            with dve.If(fast == 1):
                step0 = passes * STEPS

                def with_block(f, s, r):
                    weigh(1, step0 + f * U, f * U + (U - 1), s, CH, U, U)
                    add_block(f, r, step0 + f * U)
                    add_window(1, step0 + f * U, f * U + (U - 1), s, U, f + 1)

                def take_early(b):
                    read_nodes(b, early_ps[b % len(early_ps)])
                    tiles = slice(b * BATCH, (b + 1) * BATCH)
                    dve.wait_ge(nodes_read, BATCHES + b + 1)
                    dve.wait_ge(bias_added, 1)
                    nc.vector.tensor_tensor(h_nodes[:, tiles, :], h_nodes[:, tiles, :], x_nodes[:, tiles, :], ALU.add).then_inc(nodes_added, 1)
                    read_nodes(BATCHES, None, b)
                    for part, (b0, b1, _) in enumerate(PARTS[1]):
                        if b == b1 - 1:
                            norm_part(1, part)

                with dve.Fori(0, (FAST - PEEL) // SPAN6) as m:
                    for q in range(SPAN6):
                        with_block(m * SPAN6 + q, q % U, q % 2)
                for f in range(FAST - PEEL, ITERS):
                    with_block(f, f % U, f % 2)
                    if f in EARLY:
                        take_early(EARLY[f])
                weigh(1, step0 + ITERS * U, ITERS * U, ITERS % U, TAIL, U, U)
                add_window(1, step0 + ITERS * U, ITERS * U, ITERS % U, U, ITERS)
                take_early(BATCHES - 1)


_INS = ['x', 'src', 'dst', 'edge_type_32', 'edge_weight', 'L0_gnn_weight', 'L0_gnn_w_comp', 'L0_gnn_bias', 'L1_gnn_W', 'L1_gnn_b']
_FILL = {'src': 0, 'dst': N - 1, 'edge_type_32': 0, 'edge_weight': 0}


def kernel(**inputs):
    import numpy as _np
    import concourse.bacc as _bacc
    from concourse import mybir as _mybir
    from concourse.bass_utils import run_bass_kernel_spmd as _run

    nc = _bacc.Bacc("TRN2", target_bir_lowering=False, num_devices=1)
    arrays, args = {}, []
    for name in _INS:
        a = _np.ascontiguousarray(inputs[name])
        if name in _FILL:
            a = _np.concatenate([a, _np.full((CHUNKS * P - E,), _FILL[name], a.dtype)])
        arrays[f"in_{name}"] = a
        args.append(nc.dram_tensor(f"in_{name}", a.shape, _mybir.dt.from_np(a.dtype), kind="ExternalInput").ap())
    y = nc.dram_tensor("out_y", (N, D), _mybir.dt.float32, kind="ExternalOutput").ap()
    gnn_two_layers(nc, *args, y)
    r = _run(nc, [arrays], core_ids=[0])
    return r.results[0]["out_y"]
```
